# Optimizing a Trainium2 kernel written in Bass

```python
import numpy as np
import jax
import jax.numpy as jnp

def _softmax(x, axis=-1):
    return jax.nn.softmax(x, axis=axis)

def _gelu(x):
    return jax.nn.gelu(x, approximate=True)

def _silu(x):
    return jax.nn.silu(x)

def _sigmoid(x):
    return jax.nn.sigmoid(x)

def _layernorm(x, axis=-1, eps=1e-05):
    m = jnp.mean(x, axis=axis, keepdims=True)
    v = jnp.var(x, axis=axis, keepdims=True)
    return (x - m) / jnp.sqrt(v + eps)

def _scatter_add(tgt, idx, src, axis=0):
    return tgt.at[idx].add(src)

def _segment_sum(src, seg, n):
    return jax.ops.segment_sum(src, seg, n)
kernel_name = 'mk_flamingo_gated_d1_seqx_r4_7e32c1'

def setup_inputs(seed: int=0):
    np.random.seed(seed)
    _w = jnp.asarray

    def _rec_inputs():
        import jax
        import jax.numpy as jnp
        _rk = jax.random.key(seed)
        x = -0.0005207 + 1.001 * jax.random.normal(jax.random.fold_in(_rk, 1), (8, 256, 512), jnp.float32)
        _lenS = 256 - jax.random.randint(jax.random.fold_in(_rk, 7), (8,), 0, max(1, 256 // 4) + 1, jnp.int32)
        _lenS2 = 256 - jax.random.randint(jax.random.fold_in(_rk, 8), (8,), 0, max(1, 256 // 4) + 1, jnp.int32)
        _ctx_2048P = jax.random.normal(jax.random.fold_in(_rk, 12), (8, 16, 512), jnp.float32)
        _ctx_2048c = jax.random.dirichlet(jax.random.fold_in(_rk, 512), 0.3 * jnp.ones((16,), jnp.float32), (8, 256))
        _ctx_2048t = jnp.einsum('bsk,bkd->bsd', _ctx_2048c, _ctx_2048P)
        _ctx_2048t = _ctx_2048t * jax.lax.rsqrt(jnp.mean(jnp.square(_ctx_2048t)) + 1e-12) * 0.953939
        ctx_2048 = -5.72187e-05 + 0.999849 * (_ctx_2048t + 0.3 * jax.random.normal(jax.random.fold_in(_rk, 612), (8, 256, 512), jnp.float32))
        _validS = jnp.arange(256)[None, :] < _lenS[:, None]
        _validS2 = jnp.arange(256)[None, :] < _lenS2[:, None]
        _causal = jnp.tril(jnp.ones((256, 256), dtype=bool))
        mask_BxSx4224_bf0 = jnp.logical_not(jnp.ones((8, 256, 1056), dtype=bool))
        _g = jax.random.normal(jax.random.fold_in(_rk, 9001), (2, 1), jnp.float32)
        _g = jnp.sign(_g) * jnp.maximum(jnp.abs(_g), 1.0) + (_g == 0) * 1.0
        g_xattn = _g[0]
        g_ffn = _g[1]
        return (x, ctx_2048, mask_BxSx4224_bf0, g_xattn, g_ffn)
    x, ctx_2048, mask_BxSx4224_bf0, g_xattn, g_ffn = _rec_inputs()

    def _L0_xattn_setup():
        import jax, jax.numpy as jnp
        import numpy as np
        import math
        DIM = 512
        B, Q_LEN, KV_LEN = (8, 128, 1024)
        key = jax.random.key(seed)
        ks = jax.random.split(key, 8)
        x = jax.random.normal(ks[0], (B, Q_LEN, DIM), dtype=jnp.float32)
        mask = jnp.zeros((B, Q_LEN, KV_LEN + Q_LEN), dtype=bool)
        k_cache = jax.random.normal(ks[1], (B, KV_LEN, DIM), dtype=jnp.float32)
        v_cache = jax.random.normal(ks[2], (B, KV_LEN, DIM), dtype=jnp.float32)
        scale = 1.0 / math.sqrt(DIM)
        wq = jax.random.normal(ks[3], (DIM, DIM), dtype=jnp.float32) * scale
        wk = jax.random.normal(ks[4], (DIM, DIM), dtype=jnp.float32) * scale
        wv = jax.random.normal(ks[5], (DIM, DIM), dtype=jnp.float32) * scale
        wo = jax.random.normal(ks[6], (DIM, DIM), dtype=jnp.float32) * scale
        return {'x': x, 'mask': mask, 'k_cache': k_cache, 'v_cache': v_cache, 'wq': wq, 'wk': wk, 'wv': wv, 'wo': wo}
    _L0_xattn_all = _L0_xattn_setup()
    _L0_xattn_in = {k: v for k, v in _L0_xattn_all.items() if k in ('wq', 'wk', 'wv', 'wo')}
    del _L0_xattn_all

    def _L0_ffn_setup():
        import jax, jax.numpy as jnp
        import numpy as np
        TOP_K = 8
        NEG_INF = -1000000000.0
        key = jax.random.key(seed)
        ks = jax.random.split(key, 6)
        B, S, H, I, E, G, GS = (1, 512, 512, 352, 64, 8, 8)
        sc = 0.02
        return {'hidden_states': jax.random.normal(ks[0], (B, S, H), jnp.float32), 'gate_w': jax.random.normal(ks[1], (E, H), jnp.float32) * sc, 'mask_up_w': jax.random.normal(ks[2], (G, H, GS), jnp.float32) * sc, 'gate_proj_w': jax.random.normal(ks[3], (G, I, H), jnp.float32) * sc, 'up_proj_w': jax.random.normal(ks[4], (G, I, H), jnp.float32) * sc, 'down_proj_w': jax.random.normal(ks[5], (G, H, I), jnp.float32) * sc, 'inv_map': jnp.arange(G * GS, dtype=jnp.int64).reshape(G, GS)}
    _L0_ffn_all = _L0_ffn_setup()
    _L0_ffn_in = {k: v for k, v in _L0_ffn_all.items() if k in ('gate_w', 'mask_up_w', 'gate_proj_w', 'up_proj_w', 'down_proj_w', 'inv_map')}
    del _L0_ffn_all
    return {'x': x, 'ctx_2048': ctx_2048, 'mask_BxSx4224_bf0': mask_BxSx4224_bf0, 'g_xattn': g_xattn, 'g_ffn': g_ffn, 'L0_xattn_wq': _L0_xattn_in['wq'], 'L0_xattn_wk': _L0_xattn_in['wk'], 'L0_xattn_wv': _L0_xattn_in['wv'], 'L0_xattn_wo': _L0_xattn_in['wo'], 'L0_ffn_gate_w': _L0_ffn_in['gate_w'], 'L0_ffn_mask_up_w': _L0_ffn_in['mask_up_w'], 'L0_ffn_gate_proj_w': _L0_ffn_in['gate_proj_w'], 'L0_ffn_up_proj_w': _L0_ffn_in['up_proj_w'], 'L0_ffn_down_proj_w': _L0_ffn_in['down_proj_w'], 'L0_ffn_inv_map': _L0_ffn_in['inv_map']}

def reference(x, ctx_2048, mask_BxSx4224_bf0, g_xattn, g_ffn, L0_xattn_wq, L0_xattn_wk, L0_xattn_wv, L0_xattn_wo, L0_ffn_gate_w, L0_ffn_mask_up_w, L0_ffn_gate_proj_w, L0_ffn_up_proj_w, L0_ffn_down_proj_w, L0_ffn_inv_map):
    import jax
    import jax.numpy as jnp

    def _L0_xattn_ref(x, mask, k_cache, v_cache, wq, wk, wv, wo):
        import jax, jax.numpy as jnp
        import numpy as np
        import math
        DIM = 512
        B, Q_LEN, KV_LEN = (8, 128, 1024)
        q = jnp.einsum('bsd,ed->bse', x, wq)
        k_new = jnp.einsum('bsd,ed->bse', x, wk)
        v_new = jnp.einsum('bsd,ed->bse', x, wv)
        k = jnp.concatenate([k_cache, k_new], axis=1)
        v = jnp.concatenate([v_cache, v_new], axis=1)
        scale = 1.0 / math.sqrt(q.shape[-1])
        scores = jnp.einsum('bqd,bkd->bqk', q, k) * scale
        attn = jax.nn.softmax(scores, axis=-1)
        out = jnp.einsum('bqk,bkd->bqd', attn, v)
        return jnp.einsum('bqd,ed->bqe', out, wo)

    def _L0_ffn_ref(hidden_states, gate_w, mask_up_w, gate_proj_w, up_proj_w, down_proj_w, inv_map):
        import jax, jax.numpy as jnp
        import numpy as np
        TOP_K = 8
        NEG_INF = -1000000000.0
        B, S, H = hidden_states.shape
        x = hidden_states.reshape(-1, H)
        N = x.shape[0]
        E = gate_w.shape[0]
        scores = jax.nn.softmax(x @ gate_w.T, axis=-1)
        topk_w, topk_idx = jax.lax.top_k(scores, TOP_K)
        w_e = jnp.zeros((N, E), x.dtype).at[jnp.arange(N)[:, None], topk_idx].add(topk_w)
        flat = w_e[:, inv_map]
        scalar = flat.sum(-1)
        soft = jax.nn.softmax(jnp.where(flat == 0, NEG_INF, flat), axis=-1)
        xg = x[:, None, :] + jnp.einsum('ngi,ghi->ngh', soft, mask_up_w)
        g = jnp.einsum('ngh,gih->ngi', xg, gate_proj_w)
        u = jnp.einsum('ngh,gih->ngi', xg, up_proj_w)
        a = jax.nn.silu(g) * u
        d = jnp.einsum('ngi,ghi->ngh', a, down_proj_w)
        y = jnp.einsum('ng,ngh->nh', scalar, d)
        return y.reshape(B, S, H)
    x = x + jnp.tanh(g_xattn[0]) * _L0_xattn_ref(_layernorm(x, axis=-1), mask_BxSx4224_bf0, ctx_2048, ctx_2048, L0_xattn_wq, L0_xattn_wk, L0_xattn_wv, L0_xattn_wo)
    x = x + jnp.tanh(g_ffn[0]) * _L0_ffn_ref(_layernorm(x, axis=-1), L0_ffn_gate_w, L0_ffn_mask_up_w, L0_ffn_gate_proj_w, L0_ffn_up_proj_w, L0_ffn_down_proj_w, L0_ffn_inv_map)
    return x

_drawn_inputs = setup_inputs


def setup_inputs(seed=0):
    import zlib

    import numpy as np

    out = dict(_drawn_inputs(seed))
    spreads = {}
    factors = {'L0_ffn_gate_w': 8.0,
     'L0_ffn_mask_up_w': 8.0,
     'L0_ffn_gate_proj_w': 7.238,
     'L0_ffn_up_proj_w': 7.29,
     'L0_ffn_down_proj_w': 7.099}
    for name, (base, spread) in spreads.items():
        noise = np.random.default_rng([zlib.crc32(name.encode()), seed]).standard_normal(out[name].shape)
        drawn = base * np.exp(spread * noise) if base else spread * noise
        out[name] = jnp.asarray(drawn.astype(out[name].dtype))
    for name, factor in factors.items():
        out[name] = (out[name] * factor).astype(out[name].dtype)
    return out
```

```python
from contextlib import ExitStack

import concourse.bass as bass
from concourse import mybir

ALU = mybir.AluOpType
ACT = mybir.ActivationFunctionType
AX = mybir.AxisListType
F32 = mybir.dt.float32
F32R = mybir.dt.float32r
BF16 = mybir.dt.bfloat16
I32 = mybir.dt.int32

P = 128
B, S, D = 8, 256, 512
DT = D // P
ST = S // P
NT = B * ST
N = B * S
KEYS = 2 * S
KT = KEYS // P
BANK = 512
CH = N // BANK
E, G, GS, INNER = 64, 8, 8, 352
HALF_E = E // 2
HALF_G = G // 2
PAIRS = G * INNER // P // 2
HALF_ROWS = HALF_G * INNER
SOFT_ROWS = 3 * HALF_E
STACK = SOFT_ROWS + 2 * HALF_G
SCALE = float(D) ** -0.5
EPS = 1e-5
NEG_INF = -1e9
RSQRT_SEED = float(0x5F3759DF)
NEWTON = 4


def f32(ap):
    return ap.bitcast(F32)


def split_products(hi_l, lo_l, hi_r, lo_r, tiles):
    return [pair for k in tiles for pair in
            ((lo_l(k), hi_r(k)), (hi_l(k), lo_r(k)), (hi_l(k), hi_r(k)))]


def accumulate(nc, out, pairs):
    for n, (stationary, moving) in enumerate(pairs):
        last = nc.tensor.matmul(out, stationary, moving, start=n == 0, stop=n == len(pairs) - 1)
    return last


def layer_program(nc, x, ctx_nat, ctx_t, w_qkvo, w_gate_up, w_down, mask_up, gate_t, inv_map, gains, out):
    with ExitStack() as stack:
        def sem(name):
            return stack.enter_context(nc.semaphore(name))

        def sb(where, name, shape, dt):
            return where.enter_context(nc.sbuf_tensor(name, shape, dt))

        xres = sb(stack, "xres", [P, NT, D], F32)
        ident = sb(stack, "ident", [P, P], F32)
        group_mask = sb(stack, "group_mask", [STACK, HALF_ROWS], BF16)
        mu_hi = sb(stack, "mu_hi", [P, DT, 2, SOFT_ROWS], F32R)
        mu_lo = sb(stack, "mu_lo", [P, DT, 2, SOFT_ROWS], F32R)
        gate_hi = sb(stack, "gate_hi", [P, DT, E], F32R)
        gate_lo = sb(stack, "gate_lo", [P, DT, E], F32R)
        stats_x = sb(stack, "stats_x", [P, NT, 6], F32)
        mv = sb(stack, "mv", [P, NT, 2], F32)
        var_eps = sb(stack, "var_eps", [P, NT], F32)
        newton = sb(stack, "newton", [P, NT], F32)
        rstd = sb(stack, "rstd", [P, NT], F32)
        seed = sb(stack, "seed", [P, NT], I32)
        gains_raw = sb(stack, "gains_raw", [P, 2], F32)
        gain = sb(stack, "gain", [P, 2], F32)
        neg_max = sb(stack, "neg_max", [P, ST], F32)
        exp_bias = sb(stack, "exp_bias", [P, ST], F32)
        row_sum = sb(stack, "row_sum", [P, ST], F32)
        row_inv = sb(stack, "row_inv", [P, ST], F32)
        out_coef = sb(stack, "out_coef", [P, ST], F32)
        inv_raw = sb(stack, "inv_raw", [E, E], I32)
        inv_f = sb(stack, "inv_f", [E, E], F32)
        inv_neg = sb(stack, "inv_neg", [E, E], F32)
        expert_i = sb(stack, "expert_i", [E, 1], I32)
        expert_f = sb(stack, "expert_f", [E, 1], F32)
        pick = sb(stack, "pick", [E, E], F32)
        row_i = sb(stack, "row_i", [STACK, 1], I32)
        row_group_i = sb(stack, "row_group_i", [STACK, 1], I32)
        row_group = sb(stack, "row_group", [STACK, 1], F32)

        a = ExitStack()
        w_hi = sb(a, "w_hi", [P, 4, DT, D], F32R)
        w_lo = sb(a, "w_lo", [P, 4, DT, D], F32R)
        xnt_hi = sb(a, "xnt_hi", [P, DT, S], F32R)
        xnt_lo = sb(a, "xnt_lo", [P, DT, S], F32R)
        qt_hi = sb(a, "qt_hi", [P, DT, S], F32R)
        qt_lo = sb(a, "qt_lo", [P, DT, S], F32R)
        kt_hi = sb(a, "kt_hi", [P, DT, KEYS], F32R)
        kt_lo = sb(a, "kt_lo", [P, DT, KEYS], F32R)
        v_hi = sb(a, "v_hi", [P, KT, D], F32R)
        v_lo = sb(a, "v_lo", [P, KT, D], F32R)
        ot_hi = sb(a, "ot_hi", [P, DT, S], F32R)
        ot_lo = sb(a, "ot_lo", [P, DT, S], F32R)
        ctxt_raw = sb(a, "ctxt_raw", [P, DT, S], F32)
        ctx_raw = sb(a, "ctx_raw", [P, ST, D], F32)
        xn = sb(a, "xn", [P, ST, D], F32)
        mu_raw = sb(a, "mu_raw", [P, DT, 2, SOFT_ROWS], F32)
        gate_raw = sb(a, "gate_raw", [P, DT, E], F32)
        with ExitStack() as setup:
            w_raw = sb(setup, "w_raw", [P, 2, DT, D], F32)
            col_group = sb(setup, "col_group", [STACK, HALF_ROWS], I32)
        pt_hi = sb(a, "pt_hi", [P, KT, S], F32R)
        pt_lo = sb(a, "pt_lo", [P, KT, S], F32R)
        probs = sb(a, "probs", [P, ST, KEYS], F32)
        a.close()

        f = stack.enter_context(ExitStack())
        x2t_hi = sb(f, "x2t_hi", [P, DT, N], F32R)
        x2t_lo = sb(f, "x2t_lo", [P, DT, N], F32R)
        soft_t = sb(f, "soft_t", [STACK, 2, N], F32R)
        wgu_raw = sb(f, "wgu_raw", [P, 2, DT, 2 * P], F32)
        wd_raw = sb(f, "wd_raw", [P, 2, D], F32)
        wgu_hi = sb(f, "wgu_hi", [P, 2, DT, 2 * P], F32R)
        wgu_lo = sb(f, "wgu_lo", [P, 2, DT, 2 * P], F32R)
        with ExitStack() as normed:
            xn2 = sb(normed, "xn2", [P, NT, D], F32)
        with ExitStack() as r:
            prob = sb(r, "prob", [P, NT, E], F32)
            top8 = sb(r, "top8", [P, NT, 8], F32)
            rest = sb(r, "rest", [P, NT, E], F32)
            flat_buf = sb(r, "flat", [P, NT, E], F32)
            soft_buf = sb(r, "soft", [P, NT, E], F32)
            tok_max = sb(r, "tok_max", [P, NT], F32)
            tok_sum = sb(r, "tok_sum", [P, NT], F32)
            tok_inv = sb(r, "tok_inv", [P, NT], F32)
            grp_max = sb(r, "grp_max", [P, NT * G], F32)
            grp_sum = sb(r, "grp_sum", [P, NT * G], F32)
            grp_inv = sb(r, "grp_inv", [P, NT * G], F32)
            scal = sb(r, "scal", [P, NT, 2, HALF_G], F32)
            we_t = sb(r, "we_t", [E, N], F32)
            stack_tok = sb(r, "stack_tok", [P, NT, 2, STACK], F32R)
        flat, soft = flat_buf[:], soft_buf[:]
        wd_hi = sb(f, "wd_hi", [P, 2, D], F32R)
        wd_lo = sb(f, "wd_lo", [P, 2, D], F32R)
        at_hi = sb(f, "at_hi", [P, 2, N], F32R)
        at_lo = sb(f, "at_lo", [P, 2, N], F32R)
        silu_g = sb(f, "silu_g", [P, 2, BANK], F32)
        act = sb(f, "act", [P, 2, BANK], F32)
        a_tmp = sb(f, "a_tmp", [SOFT_ROWS, 2, P], F32)
        a_stack = sb(f, "a_stack", [SOFT_ROWS, 2, 2, P], F32R)
        pick_group = sb(f, "pick_group", [STACK, P], F32R)

        bank = [stack.enter_context(nc.psum_tensor(f"bank{i}", [P, BANK], F32)) for i in range(8)]

        s_x0, s_xr, s_gains, s_small, s_mu = map(sem, ("x0_in", "xr_in", "gains_in", "small_in", "mu_in"))
        s_win = [sem("w_in0"), sem("w_in1")]
        s_ctxt_in, s_ctx_in = sem("ctxt_in"), sem("ctx_in")
        s_w_hi, s_w_lo = sem("w_hi_done"), sem("w_lo_done")
        s_gain = sem("gain_ready")
        s_const, s_ident = sem("const_steps"), sem("ident_ready")
        s_small_hi, s_small_lo = sem("small_hi"), sem("small_lo")
        s_norm = sem("norm_steps")
        s_xn, s_xnt, s_xnt_hi, s_xnt_lo = map(sem, ("xn_ready", "xnt_ready", "xnt_hi_done", "xnt_lo_done"))
        s_q, s_q_hi, s_q_lo = map(sem, ("q_ready", "q_hi_done", "q_lo_done"))
        s_k, s_k_hi, s_k_lo = map(sem, ("k_ready", "k_hi_done", "k_lo_done"))
        s_v, s_v_hi, s_v_lo = map(sem, ("v_ready", "v_hi_done", "v_lo_done"))
        s_o, s_o_hi, s_o_lo = map(sem, ("o_ready", "o_hi_done", "o_lo_done"))
        s_pt, s_pt_hi, s_pt_lo = map(sem, ("pt_ready", "pt_hi_done", "pt_lo_done"))
        s_kc_hi, s_kc_lo, s_vc_hi, s_vc_lo = map(sem, ("kc_hi", "kc_lo", "vc_hi", "vc_lo"))
        s_scores, s_max, s_bias, s_exp = map(sem, ("scores_ready", "max_ready", "bias_ready", "exp_done"))
        s_rinv, s_coef, s_y, s_x1, s_stat = map(sem, ("row_inv_ready", "coef_ready", "y_ready", "x1_done", "x1_stats"))
        s_x2, s_x2_hi, s_x2_lo = map(sem, ("x2t_ready", "x2t_hi_done", "x2t_lo_done"))
        s_xn2, s_logit, s_route = map(sem, ("xn2_ready", "logits_ready", "route_steps"))
        s_centre, s_gexp = sem("centred"), sem("route_exp")
        s_we, s_wet, s_wet_sb, s_flat = map(sem, ("we_ready", "wet_ready", "wet_copied", "flat_ready"))
        s_soft, s_soft_hi, s_stack, s_st, s_st_sb = map(
            sem, ("soft_ready", "soft_hi_done", "stack_done", "soft_t_ready", "soft_t_copied"))
        s_fw_in = [sem("wgu_in0"), sem("wgu_in1")]
        s_fd_in = [sem("wd_in0"), sem("wd_in1")]
        s_fw_hi = [sem("wgu_hi0"), sem("wgu_hi1")]
        s_fw_lo = [sem("wgu_lo0"), sem("wgu_lo1")]
        s_fd_hi = [sem("wd_hi0"), sem("wd_hi1")]
        s_fd_lo = [sem("wd_lo0"), sem("wd_lo1")]
        s_a, s_a_masked, s_a_hi, s_a_st = map(sem, ("a_ready", "a_masked", "a_hi", "a_stack_done"))
        s_pick = sem("pick_group_done")
        s_gate, s_up, s_silu, s_prod, s_act = map(sem, ("gate_ready", "up_ready", "silu_done", "prod_done", "act_ready"))
        s_at_hi, s_at_lo = sem("at_hi_done"), sem("at_lo_done")
        s_down, s_res = sem("down_ready"), sem("residual_done")
        s_out = sem("out_stored")

        x_tiles = x.rearrange("b (t p) d -> p (b t) d", p=P)
        out_tiles = out.rearrange("b (t p) d -> p (b t) d", p=P)
        ctx_tiles = ctx_nat.rearrange("b (t p) d -> b p t d", p=P)

        block = stack.enter_context(nc.Block())

        @block.sync
        def _(sp):
            sp.dma_start(xres[:, 0:ST, :], x_tiles[:, 0:ST, :]).then_inc(s_x0, 16)
            for m in range(2):
                sp.dma_start(w_raw[:, m], w_qkvo[m]).then_inc(s_win[m], 16)
            sp.dma_start(ctxt_raw[:], ctx_t[0]).then_inc(s_ctxt_in, 16)
            sp.dma_start(ctx_raw[:], ctx_tiles[0]).then_inc(s_ctx_in, 16)
            for m in range(2, 4):
                sp.wait_ge(s_w_lo, m - 1)
                sp.dma_start(w_raw[:, m % 2], w_qkvo[m]).then_inc(s_win[m % 2], 16)
            sp.dma_start(xres[:, ST:NT, :], x_tiles[:, ST:NT, :]).then_inc(s_xr, 16)
            with sp.Fori(1, B) as b:
                sp.wait_ge(s_kc_lo, b)
                sp.dma_start(ctxt_raw[:], ctx_t[b]).then_inc(s_ctxt_in, 16)
                sp.wait_ge(s_vc_lo, b)
                sp.dma_start(ctx_raw[:], ctx_tiles[b]).then_inc(s_ctx_in, 16)
            sp.wait_ge(s_x1, NT)
            for j in range(2):
                sp.dma_start(wgu_raw[:, j], w_gate_up[0, j]).then_inc(s_fw_in[j], 16)
                sp.dma_start(wd_raw[:, j], w_down[0, j]).then_inc(s_fd_in[j], 16)
            with sp.Fori(1, PAIRS) as p:
                for j in range(2):
                    sp.wait_ge(s_fw_lo[j], p)
                    sp.dma_start(wgu_raw[:, j], w_gate_up[p, j]).then_inc(s_fw_in[j], 16)
                for j in range(2):
                    sp.wait_ge(s_fd_lo[j], p)
                    sp.dma_start(wd_raw[:, j], w_down[p, j]).then_inc(s_fd_in[j], 16)
            for b in range(B):
                sp.wait_ge(s_res, (PAIRS - 1) * NT + ST * (b + 1))
                sp.dma_start(out_tiles[:, ST * b:ST * (b + 1), :], xres[:, ST * b:ST * (b + 1), :]).then_inc(s_out, 16)
            sp.wait_ge(s_out, 16 * B)

        @block.gpsimd
        def _(pool):
            nc.gpsimd.memset(ident[:], 0.0).then_inc(s_const, 1)
            nc.gpsimd.iota(row_i[:], [[0, 1]], base=0, channel_multiplier=1).then_inc(s_const, 1)
            nc.gpsimd.iota(expert_i[:], [[0, 1]], base=0, channel_multiplier=1).then_inc(s_const, 1)
            nc.gpsimd.iota(col_group[:].rearrange("p (g i) -> p g i", g=HALF_G), [[1, HALF_G], [0, INNER]],
                           base=0, channel_multiplier=0).then_inc(s_const, 1)
            pool.wait_ge(s_const, 1)
            nc.gpsimd.affine_select(out=ident[:], in_=ident[:], compare_op=ALU.not_equal, fill=1.0, base=0,
                                    pattern=[[-1, P]], channel_multiplier=1).then_inc(s_ident, 1)

            def context_lo(b):
                pool.wait_ge(s_kc_hi, b + 1)
                nc.gpsimd.tensor_tensor(kt_lo[:, :, 0:S], ctxt_raw[:], f32(kt_hi[:, :, 0:S]),
                                        ALU.subtract).then_inc(s_kc_lo, 1)
                pool.wait_ge(s_vc_hi, b + 1)
                nc.gpsimd.tensor_tensor(v_lo[:, 0:ST, :], ctx_raw[:], f32(v_hi[:, 0:ST, :]),
                                        ALU.subtract).then_inc(s_vc_lo, 1)

            context_lo(0)
            pool.wait_ge(s_small_hi, 2)
            nc.gpsimd.tensor_tensor(mu_lo[:], mu_raw[:], f32(mu_hi[:]), ALU.subtract).then_inc(s_small_lo, 1)
            nc.gpsimd.tensor_tensor(gate_lo[:], gate_raw[:], f32(gate_hi[:]), ALU.subtract).then_inc(s_small_lo, 1)

            with pool.Fori(1, B) as b:
                context_lo(b)

            def wgu_low(p, j):
                pool.wait_ge(s_fw_hi[j], p + 1)
                nc.gpsimd.tensor_tensor(wgu_lo[:, j], wgu_raw[:, j], f32(wgu_hi[:, j]),
                                        ALU.subtract).then_inc(s_fw_lo[j], 1)

            def wd_low(p, j):
                pool.wait_ge(s_fd_hi[j], p + 1)
                nc.gpsimd.tensor_tensor(wd_lo[:, j], wd_raw[:, j], f32(wd_hi[:, j]),
                                        ALU.subtract).then_inc(s_fd_lo[j], 1)

            def act_low(p, j, c):
                n = p * 2 * CH + j * CH + c
                pool.wait_ge(s_at_hi, n + 1)
                nc.gpsimd.tensor_tensor(at_lo[:, j, c * BANK:(c + 1) * BANK], act[:, c % 2],
                                        f32(at_hi[:, j, c * BANK:(c + 1) * BANK]), ALU.subtract).then_inc(s_at_lo, 1)

            def turn(p, last):
                for j in range(2):
                    for c in range(CH):
                        act_low(p, j, c)
                        if j == 0 and c < 2:
                            wd_low(p, c)
                    if not last:
                        wgu_low(p + 1, j)

            for j in range(2):
                wgu_low(0, j)
            with pool.Fori(0, PAIRS - 1) as p:
                turn(p, False)
            turn(PAIRS - 1, True)

        @block.scalar
        def _(eng):
            nc.scalar.preload_act_table(ACT.Exp)
            eng.dma_start(gains_raw[:], gains).then_inc(s_gains, 16)
            eng.dma_start(inv_raw[:], inv_map).then_inc(s_small, 16)
            eng.dma_start(mu_raw[:], mask_up).then_inc(s_mu, 16)
            eng.dma_start(gate_raw[:], gate_t).then_inc(s_mu, 16)
            eng.wait_ge(s_gains, 16)
            nc.scalar.activation(gain[:], gains_raw[:], ACT.Tanh).then_inc(s_gain, 1)

            def weight_hi(m):
                eng.wait_ge(s_win[m % 2], 16 * (m // 2 + 1))
                nc.scalar.copy(w_hi[:, m], w_raw[:, m % 2]).then_inc(s_w_hi, 1)

            def hi_of(ready, done, value, dst, src):
                eng.wait_ge(ready, value)
                nc.scalar.copy(dst, src).then_inc(done, 1)

            def norm_hi(b):
                for j in range(2):
                    hi_of(s_xnt, s_xnt_hi, 2 * b + j + 1, xnt_hi[:, 2 * j:2 * j + 2, :], bank[2 + j][:])

            def out_hi(b):
                for j in range(2):
                    hi_of(s_o, s_o_hi, 2 * b + j + 1, ot_hi[:, 2 * j:2 * j + 2, :], bank[4 + j][:])

            def iteration(b, first=False, last=False):
                for j in range(2):
                    hi_of(s_q, s_q_hi, 2 * b + j + 1, qt_hi[:, 2 * j:2 * j + 2, :], bank[j][:])
                for j in range(2):
                    hi_of(s_k, s_k_hi, 2 * b + j + 1, kt_hi[:, 2 * j:2 * j + 2, S:KEYS], bank[2 + j][:])
                eng.wait_ge(s_ctxt_in, 16 * (b + 1))
                nc.scalar.copy(kt_hi[:, :, 0:S], ctxt_raw[:]).then_inc(s_kc_hi, 1)
                if first:
                    weight_hi(2)
                else:
                    out_hi(b - 1)
                eng.wait_ge(s_ctx_in, 16 * (b + 1))
                nc.scalar.copy(v_hi[:, 0:ST, :], ctx_raw[:]).then_inc(s_vc_hi, 1)
                for t in range(ST):
                    hi_of(s_v, s_v_hi, 2 * b + t + 1, v_hi[:, ST + t, :], bank[6 + t][:])
                if first:
                    weight_hi(3)
                    eng.wait_ge(s_w_lo, 4)
                for t in range(ST):
                    eng.wait_ge(s_bias, 2 * b + t + 1)
                    nc.scalar.activation(probs[:, t, :], bank[t][:], ACT.Exp, bias=exp_bias[:, t:t + 1],
                                         scale=SCALE, accum_out=row_sum[:, t:t + 1]).then_inc(s_exp, 1)
                if not last:
                    norm_hi(b + 1)
                for j in range(2):
                    hi_of(s_pt, s_pt_hi, 2 * b + j + 1, pt_hi[:, 2 * j:2 * j + 2, :], bank[6 + j][:])

            weight_hi(0)
            weight_hi(1)
            norm_hi(0)
            iteration(0, first=True)
            eng.wait_ge(s_mu, 32)
            nc.scalar.copy(mu_hi[:], mu_raw[:]).then_inc(s_small_hi, 1)
            nc.scalar.copy(gate_hi[:], gate_raw[:]).then_inc(s_small_hi, 1)
            with eng.Fori(1, B - 1) as b:
                iteration(b)
            iteration(B - 1, last=True)
            out_hi(B - 1)


            def wgu_high(p, j):
                eng.wait_ge(s_fw_in[j], 16 * (p + 1))
                nc.scalar.copy(wgu_hi[:, j], wgu_raw[:, j]).then_inc(s_fw_hi[j], 1)

            for m in range(DT * CH):
                c, h = m // DT, m % DT
                hi_of(s_x2, s_x2_hi, m + 1, x2t_hi[:, h, c * BANK:(c + 1) * BANK], bank[m % 4][:])
            for j in range(2):
                wgu_high(0, j)
            eng.wait_ge(s_centre, 1)
            nc.scalar.activation(prob[:], prob[:], ACT.Exp).then_inc(s_gexp, 1)
            for c in range(CH):
                eng.wait_ge(s_wet, c + 1)
                nc.scalar.copy(we_t[:, c * BANK:(c + 1) * BANK], bank[c][0:E, :]).then_inc(s_wet_sb, 1)
            eng.wait_ge(s_centre, 2)
            nc.scalar.activation(soft, soft, ACT.Exp).then_inc(s_gexp, 1)
            eng.wait_ge(s_soft, 1)
            soft_half = soft.rearrange("p t (h e) -> p t h e", h=2)
            nc.scalar.copy(stack_tok[:, :, :, 0:HALF_E], soft_half).then_inc(s_soft_hi, 1)
            nc.scalar.copy(stack_tok[:, :, :, 2 * HALF_E:SOFT_ROWS], soft_half).then_inc(s_stack, 1)
            for m in range(2 * CH):
                c, h = m // 2, m % 2
                eng.wait_ge(s_st, m + 1)
                nc.scalar.copy(soft_t[:, h, c * BANK:(c + 1) * BANK], bank[m % 4][0:STACK, :]).then_inc(s_st_sb, 1)
            nc.scalar.preload_act_table(ACT.Silu)

            def chunk(p, j, c):
                n = p * 2 * CH + j * CH + c
                eng.wait_ge(s_gate, n + 1)
                nc.scalar.activation(silu_g[:, c % 2], bank[3 * (c % 2)][:], ACT.Silu).then_inc(s_silu, 1)
                eng.wait_ge(s_act, n + 1)
                nc.scalar.copy(at_hi[:, j, c * BANK:(c + 1) * BANK], act[:, c % 2]).then_inc(s_at_hi, 1)

            def turn(p, last):
                for j in range(2):
                    for c in range(CH):
                        chunk(p, j, c)
                        if j == 0 and c < 2:
                            eng.wait_ge(s_fd_in[c], 16 * (p + 1))
                            nc.scalar.copy(wd_hi[:, c], wd_raw[:, c]).then_inc(s_fd_hi[c], 1)
                    if not last:
                        wgu_high(p + 1, j)

            with eng.Fori(0, PAIRS - 1) as p:
                turn(p, False)
            turn(PAIRS - 1, True)

        @block.vector
        def _(dve):
            norm_steps = [0]

            def step(ins):
                norm_steps[0] += 1
                ins.then_inc(s_norm, 1)
                dve.wait_ge(s_norm, norm_steps[0])

            def rsqrt_of_variance(t0, t1):
                v, y, z = var_eps[:, t0:t1], rstd[:, t0:t1], newton[:, t0:t1]
                step(nc.vector.tensor_scalar(v, mv[:, t0:t1, 1], EPS, None, ALU.add))
                step(nc.vector.tensor_scalar(seed[:, t0:t1], v.bitcast(I32), 1, None, ALU.logical_shift_right))
                step(nc.vector.tensor_scalar(seed[:, t0:t1], seed[:, t0:t1], -1.0, RSQRT_SEED, ALU.mult, ALU.add))
                step(nc.vector.tensor_copy(y, seed[:, t0:t1].bitcast(F32)))
                for _ in range(NEWTON):
                    step(nc.vector.tensor_tensor(z, y, y, ALU.mult))
                    step(nc.vector.tensor_tensor(z, z, v, ALU.mult))
                    step(nc.vector.tensor_scalar(z, z, -0.5, 1.5, ALU.mult, ALU.add))
                    step(nc.vector.tensor_tensor(y, y, z, ALU.mult))

            def norm_stats(t0, t1):
                for t in range(t0, t1):
                    last = nc.vector.bn_stats(stats_x[:, t, :], xres[:, t, :])
                step(last)
                norm_aggregate(t0, t1)

            def norm_aggregate(t0, t1):
                for t in range(t0, t1):
                    last = nc.vector.bn_aggr(mv[:, t, :], stats_x[:, t, :])
                step(last)
                rsqrt_of_variance(t0, t1)

            def norm_apply(b):
                for t in range(ST):
                    n = ST * b + t
                    nc.vector.tensor_scalar(xn[:, t, :], xres[:, bass.ds(n, 1), :], mv[:, bass.ds(n, 1), 0],
                                            rstd[:, bass.ds(n, 1)], ALU.subtract, ALU.mult).then_inc(s_xn, 1)

            def lo_of(hi_done, done, value, dst, src, hi):
                dve.wait_ge(hi_done, value)
                nc.vector.tensor_tensor(dst, src, f32(hi), ALU.subtract).then_inc(done, 1)

            def norm_lo(b):
                for j in range(2):
                    at = slice(2 * j, 2 * j + 2)
                    lo_of(s_xnt_hi, s_xnt_lo, 2 * b + j + 1, xnt_lo[:, at, :], bank[2 + j][:], xnt_hi[:, at, :])

            def out_lo(b):
                for j in range(2):
                    at = slice(2 * j, 2 * j + 2)
                    lo_of(s_o_hi, s_o_lo, 2 * b + j + 1, ot_lo[:, at, :], bank[4 + j][:], ot_hi[:, at, :])

            def weight_lo(m):
                lo_of(s_w_hi, s_w_lo, m + 1, w_lo[:, m], w_raw[:, m % 2], w_hi[:, m])

            def residual(b):
                for t in range(ST):
                    n = ST * b + t
                    row = xres[:, bass.ds(n, 1), :]
                    dve.wait_ge(s_y, n + 1)
                    nc.vector.scalar_tensor_tensor(out=row, in0=bank[4 + t][:], scalar=out_coef[:, t:t + 1], in1=row,
                                                   op0=ALU.mult, op1=ALU.add).then_inc(s_x1, 1)
                for t in range(ST):
                    n = ST * b + t
                    dve.wait_ge(s_x1, n + 1)
                    nc.vector.bn_stats(stats_x[:, bass.ds(n, 1), :], xres[:, bass.ds(n, 1), :]).then_inc(s_stat, 1)

            def coefficient(b):
                dve.wait_ge(s_exp, 2 * b + 2)
                nc.vector.reciprocal(row_inv[:], row_sum[:]).then_inc(s_rinv, 1)
                dve.wait_ge(s_rinv, b + 1)
                nc.vector.tensor_scalar(out_coef[:], row_inv[:], gain[:, 0:1], None, ALU.mult).then_inc(s_coef, 1)

            def iteration(b, first=False, last=False):
                for j in range(2):
                    at = slice(2 * j, 2 * j + 2)
                    lo_of(s_q_hi, s_q_lo, 2 * b + j + 1, qt_lo[:, at, :], bank[j][:], qt_hi[:, at, :])
                for j in range(2):
                    at = slice(2 * j, 2 * j + 2)
                    lo_of(s_k_hi, s_k_lo, 2 * b + j + 1, kt_lo[:, at, S:KEYS], bank[2 + j][:], kt_hi[:, at, S:KEYS])
                if first:
                    weight_lo(2)
                    dve.wait_ge(s_xr, 16)
                    norm_stats(ST, NT)
                else:
                    out_lo(b - 1)
                if not last:
                    norm_apply(b + 1)
                for t in range(ST):
                    lo_of(s_v_hi, s_v_lo, 2 * b + t + 1, v_lo[:, ST + t, :], bank[6 + t][:], v_hi[:, ST + t, :])
                if first:
                    weight_lo(3)
                for t in range(ST):
                    dve.wait_ge(s_scores, 2 * b + t + 1)
                    nc.vector.tensor_reduce(neg_max[:, t:t + 1], bank[t][:], AX.X, ALU.max,
                                            negate=True).then_inc(s_max, 1)
                    dve.wait_ge(s_max, 2 * b + t + 1)
                    nc.vector.tensor_scalar(exp_bias[:, t:t + 1], neg_max[:, t:t + 1], SCALE, None,
                                            ALU.mult).then_inc(s_bias, 1)
                if not last:
                    norm_lo(b + 1)
                if not first:
                    dve.wait_ge(s_coef, b)
                    residual(b - 1)
                coefficient(b)
                for j in range(2):
                    at = slice(2 * j, 2 * j + 2)
                    lo_of(s_pt_hi, s_pt_lo, 2 * b + j + 1, pt_lo[:, at, :], bank[6 + j][:], pt_hi[:, at, :])

            dve.wait_ge(s_x0, 16)
            norm_stats(0, ST)
            norm_apply(0)
            weight_lo(0)
            norm_lo(0)
            weight_lo(1)
            dve.wait_ge(s_const, 4)
            step(nc.vector.tensor_scalar(row_group_i[0:SOFT_ROWS], row_i[0:SOFT_ROWS], HALF_E - 1, 3,
                                         ALU.bitwise_and, ALU.logical_shift_right))
            step(nc.vector.tensor_scalar(row_group_i[SOFT_ROWS:STACK], row_i[SOFT_ROWS:STACK], HALF_G - 1, None,
                                         ALU.bitwise_and))
            step(nc.vector.tensor_copy(row_group[:], row_group_i[:]))
            step(nc.vector.tensor_scalar(group_mask[:], col_group[:], row_group[:, 0:1], None, ALU.is_equal))
            dve.wait_ge(s_small, 16)
            step(nc.vector.tensor_copy(inv_f[:], inv_raw[:]))
            step(nc.vector.tensor_scalar(inv_neg[:], inv_f[:], 0.0, float(E), ALU.is_lt, ALU.mult))
            step(nc.vector.tensor_tensor(inv_f[:], inv_f[:], inv_neg[:], ALU.add))
            step(nc.vector.tensor_copy(expert_f[:], expert_i[:]))
            step(nc.vector.tensor_scalar(pick[:], inv_f[:], expert_f[:, 0:1], None, ALU.is_equal))
            dve.wait_ge(s_gain, 1)
            iteration(0, first=True)
            with dve.Fori(1, B - 1) as b:
                iteration(b)
            iteration(B - 1, last=True)
            out_lo(B - 1)
            dve.wait_ge(s_coef, B)
            residual(B - 1)

            dve.wait_ge(s_stat, NT)
            norm_aggregate(0, NT)
            for t in range(NT):
                nc.vector.tensor_scalar(xn2[:, t, :], xres[:, t, :], mv[:, t, 0:1], rstd[:, t:t + 1],
                                        ALU.subtract, ALU.mult).then_inc(s_xn2, 1)
            for m in range(DT * CH):
                c, h = m // DT, m % DT
                at = slice(c * BANK, (c + 1) * BANK)
                lo_of(s_x2_hi, s_x2_lo, m + 1, x2t_lo[:, h, at], bank[m % 4][:], x2t_hi[:, h, at])

            route_steps = [0]

            def route(ins):
                route_steps[0] += 1
                ins.then_inc(s_route, 1)
                dve.wait_ge(s_route, route_steps[0])

            def bank_tiles(i):
                return bank[4 + i][:].rearrange("p (t e) -> p t e", e=E)

            def per_tile(v, t0, t1, n):
                return v[:, t0:t1].unsqueeze(2).broadcast_to([P, t1 - t0, n])

            dve.wait_ge(s_logit, 1)
            for i in range(2):
                last = nc.vector.tensor_reduce(tok_max[:, 8 * i:8 * i + 8], bank_tiles(i), AX.X, ALU.max)
            route(last)
            for i in range(2):
                last = nc.vector.tensor_tensor(prob[:, 8 * i:8 * i + 8, :], bank_tiles(i),
                                               per_tile(tok_max, 8 * i, 8 * i + 8, E), ALU.subtract)
            last.then_inc(s_centre, 1)
            dve.wait_ge(s_gexp, 1)
            route(nc.vector.tensor_reduce(tok_sum[:], prob[:], AX.X, ALU.add))
            route(nc.vector.reciprocal(tok_inv[:], tok_sum[:]))
            route(nc.vector.tensor_tensor(prob[:], prob[:], per_tile(tok_inv, 0, NT, E), ALU.mult))
            for t in range(NT):
                last = nc.vector.max(top8[:, t, :], prob[:, t, :])
            route(last)
            for t in range(NT):
                last = nc.vector.match_replace(rest[:, t, :], top8[:, t, :], prob[:, t, :], 0.0)
            route(last)
            nc.vector.tensor_tensor(rest[:], prob[:], rest[:], ALU.subtract).then_inc(s_we, 1)
            dve.wait_ge(s_flat, 1)
            for i in range(2):
                last = nc.vector.tensor_copy(flat[:, 8 * i:8 * i + 8, :], bank_tiles(i))
            route(last)
            by_group = flat.rearrange("p t (g s) -> p (t g) s", s=GS)
            soft_group = soft.rearrange("p t (g s) -> p (t g) s", s=GS)
            route(nc.vector.tensor_scalar(soft, flat, 0.0, NEG_INF, ALU.is_equal, ALU.mult))
            route(nc.vector.tensor_tensor(soft, soft, flat, ALU.add))
            route(nc.vector.tensor_reduce(grp_max[:], soft_group, AX.X, ALU.max))
            nc.vector.tensor_tensor(soft_group, soft_group, per_tile(grp_max, 0, NT * G, GS),
                                    ALU.subtract).then_inc(s_centre, 1)
            scal_flat = scal[:].rearrange("p t h g -> p (t h g)")
            route(nc.vector.tensor_reduce(scal_flat, by_group, AX.X, ALU.add))
            route(nc.vector.tensor_scalar(scal_flat, scal_flat, gain[:, 1:2], None, ALU.mult))
            scal_hi = stack_tok[:, :, :, SOFT_ROWS:SOFT_ROWS + HALF_G]
            route(nc.vector.tensor_copy(scal_hi, scal[:]))
            route(nc.vector.tensor_tensor(stack_tok[:, :, :, SOFT_ROWS + HALF_G:STACK], scal[:], f32(scal_hi),
                                          ALU.subtract))
            dve.wait_ge(s_gexp, 2)
            route(nc.vector.tensor_reduce(grp_sum[:], soft_group, AX.X, ALU.add))
            route(nc.vector.reciprocal(grp_inv[:], grp_sum[:]))
            nc.vector.tensor_tensor(soft_group, soft_group, per_tile(grp_inv, 0, NT * G, GS),
                                    ALU.mult).then_inc(s_soft, 1)
            dve.wait_ge(s_soft_hi, 1)
            nc.vector.tensor_tensor(stack_tok[:, :, :, HALF_E:2 * HALF_E],
                                    soft.rearrange("p t (h e) -> p t h e", h=2),
                                    f32(stack_tok[:, :, :, 0:HALF_E]), ALU.subtract).then_inc(s_stack, 1)

            dve.wait_ge(s_st, 2 * CH)
            nc.vector.memset(f32(pick_group[:]), 0.0).then_inc(s_pick, 1)

            def a_tile(p, j):
                k = 2 * p + j + 1
                columns = group_mask[0:SOFT_ROWS, bass.ds(p * P, P)].unsqueeze(1).broadcast_to([SOFT_ROWS, 2, P])
                dve.wait_ge(s_a, k)
                nc.vector.tensor_tensor(a_tmp[:], bank[6 + j][0:SOFT_ROWS, 0:2 * P].rearrange("p (m r) -> p m r", m=2),
                                        columns, ALU.mult).then_inc(s_a_masked, 1)
                dve.wait_ge(s_a_masked, k)
                nc.vector.tensor_copy(a_stack[:, j], a_tmp[:]).then_inc(s_a_hi, 1)
                dve.wait_ge(s_a_hi, k)
                low = slice(2 * HALF_E, SOFT_ROWS)
                nc.vector.tensor_tensor(a_stack[low, j], a_tmp[low], f32(a_stack[low, j]),
                                        ALU.subtract).then_inc(s_a_st, 1)

            def chunk(p, j, c):
                n = p * 2 * CH + j * CH + c
                s = c % 2
                dve.wait_ge(s_silu, n + 1)
                dve.wait_ge(s_up, n + 1)
                if j == 1 or c >= 2:
                    dve.wait_ge(s_at_lo, n - 1)
                nc.vector.tensor_tensor(act[:, s], silu_g[:, s], bank[3 * s + 1][:], ALU.mult).then_inc(s_prod, 1)
                dve.wait_ge(s_prod, n + 1)
                nc.vector.tensor_tensor(act[:, s], act[:, s], bank[3 * s + 2][:], ALU.mult).then_inc(s_act, 1)

            def turn(p, last):
                for j in range(2):
                    if j == 0:
                        dve.wait_ge(s_pick, p + 1)
                        nc.vector.tensor_copy(pick_group[SOFT_ROWS:STACK, :],
                                              group_mask[SOFT_ROWS:STACK, bass.ds(p * P, P)]).then_inc(s_pick, 1)
                    a_tile(p, j)
                    for c in range(CH):
                        chunk(p, j, c)
                for t in range(NT):
                    dve.wait_ge(s_down, NT * p + t + 1)
                    nc.vector.tensor_tensor(xres[:, t, :], xres[:, t, :], bank[6 + t % 2][:], ALU.add).then_inc(s_res, 1)

            with dve.Fori(0, PAIRS - 1) as p:
                turn(p, False)
            turn(PAIRS - 1, True)

        @block.tensor
        def _(pe):
            def mm(out_ap, pairs):
                return accumulate(nc, out_ap, pairs)

            def project_t(m, b0, ready):
                for e in range(DT):
                    last = mm(bank[b0 + e // 2][:, (e % 2) * S:(e % 2 + 1) * S],
                              split_products(lambda k: w_hi[:, m, k, e * P:(e + 1) * P], lambda k: w_lo[:, m, k, e * P:(e + 1) * P],
                                             lambda k: xnt_hi[:, k, :], lambda k: xnt_lo[:, k, :], range(DT)))
                    if e % 2:
                        last.then_inc(ready, 1)

            def transposes(src, b0, ready, count, columns):
                for h in range(columns):
                    for t in range(ST):
                        last = nc.tensor.transpose(bank[b0 + h // 2][:, (h % 2) * S + t * P:(h % 2) * S + (t + 1) * P],
                                                   src[:, t, h * P:(h + 1) * P], ident[:])
                    if h % 2:
                        last.then_inc(ready, 1)

            def norm_transposes(b):
                pe.wait_ge(s_xn, 2 * b + 2)
                transposes(xn, 2, s_xnt, 2, DT)

            def attend(b):
                pe.wait_ge(s_pt_lo, 2 * b + 2)
                pe.wait_ge(s_v_lo, 2 * b + 2)
                pe.wait_ge(s_vc_lo, b + 1)
                for d in range(DT):
                    at = slice(d * P, (d + 1) * P)
                    last = mm(bank[4 + d // 2][:, (d % 2) * S:(d % 2 + 1) * S],
                              split_products(lambda k: v_hi[:, k, at], lambda k: v_lo[:, k, at],
                                             lambda k: pt_hi[:, k, :], lambda k: pt_lo[:, k, :], range(KT)))
                    if d % 2:
                        last.then_inc(s_o, 1)

            def project_out(b):
                pe.wait_ge(s_o_lo, 2 * b + 2)
                for t in range(ST):
                    at = slice(t * P, (t + 1) * P)
                    mm(bank[4 + t][:], split_products(lambda k: ot_hi[:, k, at], lambda k: ot_lo[:, k, at],
                                                      lambda k: w_hi[:, 3, k, :], lambda k: w_lo[:, 3, k, :],
                                                      range(DT))).then_inc(s_y, 1)

            def iteration(b, first=False, last=False):
                pe.wait_ge(s_xnt_lo, 2 * b + 2)
                pe.wait_ge(s_exp, 2 * b)
                if first:
                    pe.wait_ge(s_w_lo, 1)
                project_t(0, 0, s_q)
                if first:
                    pe.wait_ge(s_w_lo, 2)
                project_t(1, 2, s_k)
                if first:
                    pe.wait_ge(s_w_lo, 3)
                else:
                    attend(b - 1)
                pe.wait_ge(s_pt_lo, 2 * b)
                for t in range(ST):
                    at = slice(t * P, (t + 1) * P)
                    mm(bank[6 + t][:], split_products(lambda k: xnt_hi[:, k, at], lambda k: xnt_lo[:, k, at],
                                                      lambda k: w_hi[:, 2, k, :], lambda k: w_lo[:, 2, k, :],
                                                      range(DT))).then_inc(s_v, 1)
                pe.wait_ge(s_q_lo, 2 * b + 2)
                pe.wait_ge(s_k_lo, 2 * b + 2)
                pe.wait_ge(s_kc_lo, b + 1)
                for t in range(ST):
                    at = slice(t * P, (t + 1) * P)
                    mm(bank[t][:], split_products(lambda k: qt_hi[:, k, at], lambda k: qt_lo[:, k, at],
                                                  lambda k: kt_hi[:, k, :], lambda k: kt_lo[:, k, :],
                                                  range(DT))).then_inc(s_scores, 1)
                if not last:
                    norm_transposes(b + 1)
                if first:
                    pe.wait_ge(s_w_lo, 4)
                else:
                    project_out(b - 1)
                pe.wait_ge(s_exp, 2 * b + 2)
                pe.wait_ge(s_v_lo, 2 * b + 2)
                transposes(probs, 6, s_pt, 2, KT)

            pe.wait_ge(s_ident, 1)
            norm_transposes(0)
            iteration(0, first=True)
            with pe.Fori(1, B - 1) as b:
                iteration(b)
            iteration(B - 1, last=True)
            attend(B - 1)
            project_out(B - 1)

            pe.wait_ge(s_pt_lo, 2 * B)
            for m in range(DT * CH):
                c, h = m // DT, m % DT
                pe.wait_ge(s_xn2, 4 * c + 4)
                if m >= 4:
                    pe.wait_ge(s_x2_lo, m - 3)
                for t in range(4):
                    last = nc.tensor.transpose(bank[m % 4][:, t * P:(t + 1) * P],
                                               xn2[:, 4 * c + t, h * P:(h + 1) * P], ident[:])
                last.then_inc(s_x2, 1)
            pe.wait_ge(s_small_lo, 2)
            pe.wait_ge(s_x1, NT)
            for t in range(NT):
                pe.wait_ge(s_x2_lo, DT * (t // 4 + 1))
                at = slice(t * P, (t + 1) * P)
                last = mm(bank[4 + t // 8][:, (t % 8) * E:(t % 8 + 1) * E],
                          split_products(lambda k: x2t_hi[:, k, at], lambda k: x2t_lo[:, k, at],
                                         lambda k: gate_hi[:, k, :], lambda k: gate_lo[:, k, :], range(DT)))
            last.then_inc(s_logit, 1)
            pe.wait_ge(s_we, 1)
            for c in range(CH):
                for t in range(4):
                    last = nc.tensor.transpose(bank[c][0:E, t * P:(t + 1) * P], rest[:, 4 * c + t, :], ident[:])
                last.then_inc(s_wet, 1)
            for t in range(NT):
                pe.wait_ge(s_wet_sb, t // 4 + 1)
                last = nc.tensor.matmul(bank[4 + t // 8][:, (t % 8) * E:(t % 8 + 1) * E],
                                        we_t[:, t * P:(t + 1) * P], pick[:], start=True, stop=True)
            last.then_inc(s_flat, 1)
            pe.wait_ge(s_stack, 2)
            for m in range(2 * CH):
                c, h = m // 2, m % 2
                if m >= 4:
                    pe.wait_ge(s_st_sb, m - 3)
                for t in range(4):
                    last = nc.tensor.transpose(bank[m % 4][0:STACK, t * P:(t + 1) * P],
                                               f32(stack_tok[:, 4 * c + t, h, :]), ident[:])
                last.then_inc(s_st, 1)
            pe.wait_ge(s_st_sb, 2 * CH)

            def a_products(p, j):
                pe.wait_ge(s_pick, p + 2)
                mm(bank[6 + j][0:SOFT_ROWS, 0:2 * P],
                   split_products(lambda k: mu_hi[:, k, j, :], lambda k: mu_lo[:, k, j, :],
                                  lambda k: wgu_hi[:, j, k, :], lambda k: wgu_lo[:, j, k, :],
                                  range(DT))).then_inc(s_a, 1)

            def chunk(p, j, c):
                n = p * 2 * CH + j * CH + c
                at = slice(c * BANK, (c + 1) * BANK)
                b0 = 3 * (c % 2)
                if j == 1 or c >= 2:
                    pe.wait_ge(s_act, n - 1)
                if c == 0:
                    pe.wait_ge(s_fw_lo[j], p + 1)
                for m in range(2):
                    rows = slice(m * P, (m + 1) * P)
                    pairs = split_products(lambda k: wgu_hi[:, j, k, rows], lambda k: wgu_lo[:, j, k, rows],
                                           lambda k: x2t_hi[:, k, at], lambda k: x2t_lo[:, k, at], range(DT))
                    for q, (stationary, moving) in enumerate(pairs):
                        nc.tensor.matmul(bank[b0 + m][:], stationary, moving, start=q == 0, stop=False)
                    if c == 0 and m == 0:
                        a_products(p, j)
                    if c > 0:
                        soft_product(j, c, m)
                if c == 0:
                    pe.wait_ge(s_a_st, 2 * p + j + 1)
                    for m in range(2):
                        soft_product(j, c, m)
                nc.tensor.matmul(bank[b0 + 2][:], pick_group[:], soft_t[:, j, at], start=True, stop=True).then_inc(s_up, 1)

            def soft_product(j, c, m):
                last = nc.tensor.matmul(bank[3 * (c % 2) + m][:], a_stack[:, j, m, :],
                                        soft_t[0:SOFT_ROWS, j, c * BANK:(c + 1) * BANK], start=False, stop=True)
                if m == 0:
                    last.then_inc(s_gate, 1)

            def turn(p, last):
                for j in range(2):
                    for c in range(CH):
                        chunk(p, j, c)
                for j in range(2):
                    pe.wait_ge(s_fd_lo[j], p + 1)
                for t in range(NT):
                    pe.wait_ge(s_at_lo, 2 * CH * p + CH + t // 4 + 1)
                    if t >= 2:
                        pe.wait_ge(s_res, NT * p + t - 1)
                    at = slice(t * P, (t + 1) * P)
                    mm(bank[6 + t % 2][:], split_products(lambda k: at_hi[:, k, at], lambda k: at_lo[:, k, at],
                                                          lambda k: wd_hi[:, k, :], lambda k: wd_lo[:, k, :],
                                                          range(2))).then_inc(s_down, 1)

            with pe.Fori(0, PAIRS - 1) as p:
                turn(p, False)
            turn(PAIRS - 1, True)


def kernel(**inputs):
    import numpy as np
    import concourse.bacc as bacc
    from concourse.bass_utils import run_bass_kernel_spmd

    given = {name: np.asarray(value) for name, value in inputs.items()}

    def by_k_tile(w):
        return w.T.reshape(DT, P, w.shape[0]).transpose(1, 0, 2)

    w_qkvo = np.stack([by_k_tile(given[f"L0_xattn_w{n}"]) for n in "qkvo"])
    ctx = given["ctx_2048"]
    ctx_t = ctx.transpose(0, 2, 1).reshape(B, DT, P, S).transpose(0, 2, 1, 3)

    def inner_rows(w):
        return w.reshape(2, PAIRS, P, D).transpose(1, 0, 2, 3)

    gate_up = np.stack([inner_rows(given[f"L0_ffn_{n}_proj_w"]) for n in ("gate", "up")], axis=2)
    gate_up = gate_up.reshape(PAIRS, 2, 2, P, DT, P).transpose(0, 1, 5, 4, 2, 3).reshape(PAIRS, 2, P, DT, 2 * P)
    down = inner_rows(given["L0_ffn_down_proj_w"].transpose(0, 2, 1).reshape(G * INNER, D))
    mask_up = given["L0_ffn_mask_up_w"].transpose(1, 0, 2).reshape(DT, P, 2, 1, HALF_E).transpose(1, 0, 2, 3, 4)
    mask_up = np.broadcast_to(mask_up, (P, DT, 2, 3, HALF_E)).reshape(P, DT, 2, SOFT_ROWS)
    arrays = {
        "x": given["x"],
        "ctx": ctx,
        "ctx_t": ctx_t,
        "w_qkvo": w_qkvo,
        "w_gate_up": gate_up,
        "w_down": down,
        "mask_up": mask_up,
        "gate_t": by_k_tile(given["L0_ffn_gate_w"]),
        "inv_map": np.broadcast_to(given["L0_ffn_inv_map"].reshape(1, E), (E, E)),
        "gains": np.broadcast_to(np.concatenate([given["g_xattn"], given["g_ffn"]]), (P, 2)),
    }
    arrays = {f"in_{name}": np.ascontiguousarray(value) for name, value in arrays.items()}
    nc = bacc.Bacc("TRN2", target_bir_lowering=False, num_devices=1)
    args = [nc.dram_tensor(name, value.shape, mybir.dt.from_np(value.dtype), kind="ExternalInput").ap()
            for name, value in arrays.items()]
    out = nc.dram_tensor("out", (B, S, D), F32, kind="ExternalOutput").ap()
    layer_program(nc, *args, out)
    result = run_bass_kernel_spmd(nc, [arrays], core_ids=[0])
    return result.results[0]["out"]
```

```python
from contextlib import ExitStack

import concourse.bass as bass
from concourse import mybir

ALU = mybir.AluOpType
ACT = mybir.ActivationFunctionType
AX = mybir.AxisListType
F32 = mybir.dt.float32
F32R = mybir.dt.float32r
I32 = mybir.dt.int32

P = 128
B, S, D = 8, 256, 512
DT = D // P
ST = S // P
NT = B * ST
N = B * S
KEYS = 2 * S
KT = KEYS // P
BANK = 512
CH = N // BANK
E, G, GS, INNER = 64, 8, 8, 352
HALF_E = E // 2
HALF_G = G // 2
PAIRS = G * INNER // P // 2
SLICE = P // HALF_G
SOFT_ROWS = 3 * HALF_E
STACK = SOFT_ROWS + 2 * HALF_G
SCALE = float(D) ** -0.5
EPS = 1e-5
NEG_INF = -1e9
RSQRT_SEED = float(0x5F3759DF)
NEWTON = 3
NORM_STEPS = 5 + 3 * NEWTON
ROUTE_STEPS = (1, 5, 9)
LOOP = (3, B - 1)
RING = 8


def f32(ap):
    return ap.bitcast(F32)


def split_products(hi_l, lo_l, hi_r, lo_r, tiles):
    return [pair for k in tiles for pair in
            ((lo_l(k), hi_r(k)), (hi_l(k), lo_r(k)), (hi_l(k), hi_r(k)))]


def accumulate(nc, out, pairs):
    for n, (stationary, moving) in enumerate(pairs):
        last = nc.tensor.matmul(out, stationary, moving, start=n == 0, stop=n == len(pairs) - 1)
    return last


class Steps:

    def __init__(self, engine, semaphore, per_turn):
        self.engine, self.semaphore, self.per_turn = engine, semaphore, per_turn

    def begin(self, turn):
        self.before, self.n = turn * self.per_turn, 0

    def __call__(self, instruction):
        self.n += 1
        instruction.then_inc(self.semaphore, 1)
        self.engine.wait_ge(self.semaphore, self.before + self.n)

    def end(self):
        assert self.n == self.per_turn


class Parts:

    def __init__(self, b=None):
        self.first = b == 0
        self.front = b is None or b < B
        self.next = b is None or b + 1 < B
        self.back = b is None or 1 <= b <= B
        self.route = b is None or 2 <= b <= B + 1
        self.stack = b is None or b >= 3


def layer_program(nc, x, ctx_nat, ctx_t, w_qkvo, w_gate_up, w_down, mask_up, gate_t, inv_map, gains, out):
    with ExitStack() as stack:
        def sem(name):
            return stack.enter_context(nc.semaphore(name))

        def sb(where, name, shape, dt):
            return where.enter_context(nc.sbuf_tensor(name, shape, dt))

        xres = sb(stack, "xres", [P, NT, D], F32)
        ident = sb(stack, "ident", [P, P], F32)
        group_mask = sb(stack, "group_mask", [STACK, P], F32)
        soft_t = sb(stack, "soft_t", [STACK, 2, N], F32R)
        stats_x = sb(stack, "stats_x", [P, NT, 6], F32)
        mv = sb(stack, "mv", [P, NT, 2], F32)
        var_eps = sb(stack, "var_eps", [P, NT], F32)
        newton = sb(stack, "newton", [P, NT], F32)
        rstd = sb(stack, "rstd", [P, NT], F32)
        mean_rstd = sb(stack, "mean_rstd", [P, NT], F32)
        seed = sb(stack, "seed", [P, NT], I32)
        scrap = sb(stack, "scrap", [P, 1], F32)
        stats_2 = sb(stack, "stats_2", [P, ST, 6], F32)
        mv_2 = sb(stack, "mv_2", [P, ST, 2], F32)
        rstd_2 = sb(stack, "rstd_2", [P, ST], F32)
        gains_raw = sb(stack, "gains_raw", [P, 2], F32)
        gain = sb(stack, "gain", [P, 2], F32)
        neg_max = sb(stack, "neg_max", [P, ST], F32)
        exp_bias = sb(stack, "exp_bias", [P, ST], F32)
        row_sum = sb(stack, "row_sum", [P, ST], F32)
        row_inv = sb(stack, "row_inv", [P, ST], F32)
        out_coef = sb(stack, "out_coef", [P, ST], F32)
        row_i = sb(stack, "row_i", [STACK, 1], I32)
        row_group_i = sb(stack, "row_group_i", [STACK, 1], I32)
        row_group = sb(stack, "row_group", [STACK, 1], F32)

        a = ExitStack()
        w_hi_qkv = sb(a, "w_hi_qkv", [P, 3, DT, D], F32R)
        w_lo_qkv = sb(a, "w_lo_qkv", [P, 3, DT, D], F32R)
        xnt_hi = sb(a, "xnt_hi", [P, DT, S], F32R)
        xnt_lo = sb(a, "xnt_lo", [P, DT, S], F32R)
        qt_hi = sb(a, "qt_hi", [P, DT, S], F32R)
        qt_lo = sb(a, "qt_lo", [P, DT, S], F32R)
        kt_hi = sb(a, "kt_hi", [P, DT, KEYS], F32R)
        kt_lo = sb(a, "kt_lo", [P, DT, KEYS], F32R)
        w_hi_o = sb(a, "w_hi_o", [P, DT, D], F32R)
        with ExitStack() as early:
            wv_raw = sb(early, "wv_raw", [P, DT, D], F32)
        w_lo_o = sb(a, "w_lo_o", [P, DT, D], F32R)
        v_hi = sb(a, "v_hi", [P, KT, D], F32R)
        v_lo = sb(a, "v_lo", [P, KT, D], F32R)
        ctxt_raw = sb(a, "ctxt_raw", [P, DT, S], F32)
        ctx_raw = sb(a, "ctx_raw", [P, ST, D], F32)
        gate_hi = sb(a, "gate_hi", [P, DT, E], F32R)
        gate_lo = sb(a, "gate_lo", [P, DT, E], F32R)
        inv_raw = sb(a, "inv_raw", [E, E], I32)
        inv_f = sb(a, "inv_f", [E, E], F32)
        inv_neg = sb(a, "inv_neg", [E, E], F32)
        expert_i = sb(a, "expert_i", [E, 1], I32)
        expert_f = sb(a, "expert_f", [E, 1], F32)
        pick = sb(a, "pick", [E, E], F32)
        with ExitStack() as setup:
            w_raw = sb(setup, "w_raw", [P, 2, DT, D], F32)
            col_group = sb(setup, "col_group", [STACK, P], I32)
            gate_raw = sb(setup, "gate_raw", [P, DT, E], F32)
        pt_hi = sb(a, "pt_hi", [P, KT, S], F32R)
        pt_lo = sb(a, "pt_lo", [P, KT, S], F32R)
        probs = sb(a, "probs", [P, ST, KEYS], F32)
        ot_hi = sb(a, "ot_hi", [P, DT, S], F32R)
        ot_lo = sb(a, "ot_lo", [P, DT, S], F32R)
        prob = sb(a, "prob", [P, ST, E], F32)
        top8 = sb(a, "top8", [P, ST, 8], F32)
        rest = sb(a, "rest", [P, ST, E], F32)
        flat_buf = sb(a, "flat", [P, ST, E], F32)
        soft_buf = sb(a, "soft", [P, ST, E], F32)
        tok_max = sb(a, "tok_max", [P, ST], F32)
        tok_sum = sb(a, "tok_sum", [P, ST], F32)
        tok_inv = sb(a, "tok_inv", [P, ST], F32)
        grp_max = sb(a, "grp_max", [P, ST * G], F32)
        grp_sum = sb(a, "grp_sum", [P, ST * G], F32)
        grp_inv = sb(a, "grp_inv", [P, ST * G], F32)
        scal = sb(a, "scal", [P, ST, 2, HALF_G], F32)
        logit_t = sb(a, "logit_t", [E, S], F32)
        we_t = sb(a, "we_t", [E, S], F32)
        stack_tok = sb(a, "stack_tok", [P, ST, 2, STACK], F32R)
        xn = sb(a, "xn", [P, ST, D], F32)
        a.close()
        flat, soft = flat_buf[:], soft_buf[:]

        f = stack.enter_context(ExitStack())
        x2t_hi = sb(f, "x2t_hi", [P, DT, N], F32R)
        x2t_lo = sb(f, "x2t_lo", [P, DT, N], F32R)
        with ExitStack() as before_scalars:
            xn2 = sb(before_scalars, "xn2", [P, RING, D], F32)
        scalars = sb(f, "scalars", [P, 2, N], F32)
        mu_hi = sb(f, "mu_hi", [P, DT, 2, SOFT_ROWS], F32R)
        mu_lo = sb(f, "mu_lo", [P, DT, 2, SOFT_ROWS], F32R)
        wd_hi = sb(f, "wd_hi", [P, 2, D], F32R)
        wd_lo = sb(f, "wd_lo", [P, 2, D], F32R)
        a_stack = sb(f, "a_stack", [SOFT_ROWS, 2, 2, P], F32R)
        wgu_hi = sb(f, "wgu_hi", [P, 2, DT, 2 * P], F32R)
        wgu_lo = sb(f, "wgu_lo", [P, 2, DT, 2 * P], F32R)
        wgu_raw = sb(f, "wgu_raw", [P, DT, 2 * P], F32)
        wd_raw = sb(f, "wd_raw", [P, D], F32)
        a_tmp = sb(f, "a_tmp", [SOFT_ROWS, 2, P], F32)
        pick_group = sb(f, "pick_group", [STACK, P], F32R)
        act = sb(f, "act", [P, 2, BANK], F32)
        with ExitStack() as before_ffn:
            mu_raw = sb(before_ffn, "mu_raw", [P, DT, 2, SOFT_ROWS], F32)
        at_hi = sb(f, "at_hi", [P, 2, N], F32R)
        at_lo = sb(f, "at_lo", [P, 2, N], F32R)

        bank = [stack.enter_context(nc.psum_tensor(f"bank{i}", [P, BANK], F32)) for i in range(8)]

        s_x0, s_xr, s_gains, s_small, s_mu = map(sem, ("x0_in", "xr_in", "gains_in", "small_in", "mu_in"))
        s_win = [sem(f"w_in{m}") for m in range(4)]
        s_ctxt_in, s_ctx_in = sem("ctxt_in"), sem("ctx_in")
        s_w_hi, s_w_lo = sem("w_hi_done"), sem("w_lo_done")
        s_gain = sem("gain_ready")
        s_const, s_ident = sem("const_steps"), sem("ident_ready")
        s_gate_hi, s_gate_lo, s_gate_in = sem("gate_w_hi"), sem("gate_w_lo"), sem("gate_w_in")
        s_norm = sem("norm_steps")
        s_xn, s_xnt, s_xnt_hi, s_xnt_lo = map(sem, ("xn_ready", "xnt_ready", "xnt_hi_done", "xnt_lo_done"))
        s_q, s_q_hi, s_q_lo = map(sem, ("q_ready", "q_hi_done", "q_lo_done"))
        s_k, s_k_hi, s_k_lo = map(sem, ("k_ready", "k_hi_done", "k_lo_done"))
        s_v, s_v_hi, s_v_lo = map(sem, ("v_ready", "v_hi_done", "v_lo_done"))
        s_o, s_o_hi, s_o_lo = map(sem, ("o_ready", "o_hi_done", "o_lo_done"))
        s_pt, s_pt_hi, s_pt_lo = map(sem, ("pt_ready", "pt_hi_done", "pt_lo_done"))
        s_kc_hi, s_kc_lo, s_vc_hi, s_vc_lo = map(sem, ("kc_hi", "kc_lo", "vc_hi", "vc_lo"))
        s_scores, s_max, s_bias, s_exp = map(sem, ("scores_ready", "max_ready", "bias_ready", "exp_done"))
        s_rinv, s_coef, s_y, s_x1, s_stat = map(sem, ("row_inv_ready", "coef_ready", "y_ready", "x1_done", "x1_stats"))
        s_norm2, s_xn2, s_mv = map(sem, ("norm2_steps", "xn2_ready", "mv_saved"))
        s_x2, s_x2_hi, s_x2_lo = map(sem, ("x2_ready", "x2_hi_done", "x2_lo_done"))
        s_logit_t, s_logit_sb, s_logit = map(sem, ("logit_t_ready", "logit_t_copied", "logits_ready"))
        s_route = [sem(f"route_steps{i}") for i in range(3)]
        s_centre, s_exp_tok, s_gcentre, s_exp_grp = map(sem, ("centred", "exp_tokens", "group_centred", "exp_groups"))
        s_we, s_wet, s_wet_sb, s_flat = map(sem, ("we_ready", "wet_ready", "wet_copied", "flat_ready"))
        s_flat_sb, s_soft, s_soft_hi, s_stack, s_st, s_st_sb = map(
            sem, ("flat_copied", "soft_ready", "soft_hi_done", "stack_done", "soft_t_ready", "soft_t_copied"))
        s_xf, s_x2t, s_x2t_hi, s_x2t_lo = map(sem, ("ffn_xn_ready", "x2t_ready", "x2t_hi_done", "x2t_lo_done"))
        s_mu_hi, s_mu_lo = sem("mu_hi_done"), sem("mu_lo_done")
        s_fw_in = [sem("wgu_in0"), sem("wgu_in1")]
        s_fd_in = [sem("wd_in0"), sem("wd_in1")]
        s_fw_hi = [sem("wgu_hi0"), sem("wgu_hi1")]
        s_fw_lo = [sem("wgu_lo0"), sem("wgu_lo1")]
        s_fd_hi = [sem("wd_hi0"), sem("wd_hi1")]
        s_fd_lo = [sem("wd_lo0"), sem("wd_lo1")]
        s_a, s_a_masked, s_a_hi, s_a_st = map(sem, ("a_ready", "a_masked", "a_hi", "a_stack_done"))
        s_pick, s_bc, s_bc_sb = map(sem, ("pick_group_steps", "scalars_ready", "scalars_copied"))
        s_gate, s_up, s_silu, s_prod, s_act = map(sem, ("gate_ready", "up_ready", "silu_done", "prod_done", "act_ready"))
        s_at_hi, s_at_lo = sem("at_hi_done"), sem("at_lo_done")
        s_down, s_res = sem("down_ready"), sem("residual_done")
        s_out = sem("out_stored")

        x_tiles = x.rearrange("b (t p) d -> p (b t) d", p=P)
        out_tiles = out.rearrange("b (t p) d -> p (b t) d", p=P)
        ctx_tiles = ctx_nat.rearrange("b (t p) d -> b p t d", p=P)

        def w_raw_of(m):
            return wv_raw[:] if m == 2 else w_raw[:, m % 3]

        def w_hi(m):
            return w_hi_o[:] if m == 3 else w_hi_qkv[:, m]

        def w_lo(m):
            return w_lo_o[:] if m == 3 else w_lo_qkv[:, m]

        block = stack.enter_context(nc.Block())

        @block.sync
        def _(sp):
            sp.dma_start(xres[:, 0:ST, :], x_tiles[:, 0:ST, :]).then_inc(s_x0, 16)
            for m in range(2):
                sp.dma_start(w_raw_of(m), w_qkvo[m]).then_inc(s_win[m], 16)
            sp.dma_start(w_raw_of(2), w_qkvo[2]).then_inc(s_win[2], 16)
            sp.dma_start(ctxt_raw[:], ctx_t[0]).then_inc(s_ctxt_in, 16)
            sp.dma_start(ctx_raw[:], ctx_tiles[0]).then_inc(s_ctx_in, 16)
            sp.wait_ge(s_w_lo, 1)
            sp.dma_start(w_raw_of(3), w_qkvo[3]).then_inc(s_win[3], 16)
            sp.dma_start(xres[:, ST:NT, :], x_tiles[:, ST:NT, :]).then_inc(s_xr, 16)
            with sp.Fori(1, B) as b:
                sp.wait_ge(s_kc_lo, b)
                sp.dma_start(ctxt_raw[:], ctx_t[b]).then_inc(s_ctxt_in, 16)
                sp.wait_ge(s_vc_lo, b)
                sp.dma_start(ctx_raw[:], ctx_tiles[b]).then_inc(s_ctx_in, 16)
            sp.wait_ge(s_o, NT)
            sp.dma_start(wgu_raw[:], w_gate_up[0, 0]).then_inc(s_fw_in[0], 16)
            sp.dma_start(mu_raw[:], mask_up).then_inc(s_mu, 16)
            sp.dma_start(wd_raw[:], w_down[0, 0]).then_inc(s_fd_in[0], 16)
            sp.wait_ge(s_fw_lo[0], 1)
            sp.dma_start(wgu_raw[:], w_gate_up[0, 1]).then_inc(s_fw_in[1], 16)
            sp.wait_ge(s_fd_lo[0], 1)
            sp.dma_start(wd_raw[:], w_down[0, 1]).then_inc(s_fd_in[1], 16)
            with sp.Fori(1, PAIRS) as p:
                for j in range(2):
                    sp.wait_ge(s_fw_lo[1 - j], p + j)
                    sp.dma_start(wgu_raw[:], w_gate_up[p, j]).then_inc(s_fw_in[j], 16)
                for j in range(2):
                    sp.wait_ge(s_fd_lo[1 - j], p + j)
                    sp.dma_start(wd_raw[:], w_down[p, j]).then_inc(s_fd_in[j], 16)
            for b in range(B):
                sp.wait_ge(s_res, (PAIRS - 1) * NT + ST * (b + 1))
                sp.dma_start(out_tiles[:, ST * b:ST * (b + 1), :], xres[:, ST * b:ST * (b + 1), :]).then_inc(s_out, 16)
            sp.wait_ge(s_out, 16 * B)

        @block.gpsimd
        def _(pool):
            nc.gpsimd.memset(ident[:], 0.0).then_inc(s_const, 1)
            nc.gpsimd.iota(row_i[:], [[0, 1]], base=0, channel_multiplier=1).then_inc(s_const, 1)
            nc.gpsimd.iota(expert_i[:], [[0, 1]], base=0, channel_multiplier=1).then_inc(s_const, 1)
            nc.gpsimd.iota(col_group[:].rearrange("p (g i) -> p g i", g=HALF_G), [[1, HALF_G], [0, SLICE]],
                           base=0, channel_multiplier=0).then_inc(s_const, 1)
            pool.wait_ge(s_const, 1)
            nc.gpsimd.affine_select(out=ident[:], in_=ident[:], compare_op=ALU.not_equal, fill=1.0, base=0,
                                    pattern=[[-1, P]], channel_multiplier=1).then_inc(s_ident, 1)

            def context_lo(b):
                pool.wait_ge(s_kc_hi, b + 1)
                nc.gpsimd.tensor_tensor(kt_lo[:, :, 0:S], ctxt_raw[:], f32(kt_hi[:, :, 0:S]),
                                        ALU.subtract).then_inc(s_kc_lo, 1)
                pool.wait_ge(s_vc_hi, b + 1)
                nc.gpsimd.tensor_tensor(v_lo[:, 0:ST, :], ctx_raw[:], f32(v_hi[:, 0:ST, :]),
                                        ALU.subtract).then_inc(s_vc_lo, 1)

            pool.wait_ge(s_gate_hi, 1)
            nc.gpsimd.tensor_tensor(gate_lo[:], gate_raw[:], f32(gate_hi[:]), ALU.subtract).then_inc(s_gate_lo, 1)
            context_lo(0)

            with pool.Fori(1, B) as b:
                context_lo(b)

            def wgu_low(p, j):
                pool.wait_ge(s_fw_hi[j], p + 1)
                nc.gpsimd.tensor_tensor(wgu_lo[:, j], wgu_raw[:], f32(wgu_hi[:, j]),
                                        ALU.subtract).then_inc(s_fw_lo[j], 1)

            def wd_low(p, j):
                pool.wait_ge(s_fd_hi[j], p + 1)
                nc.gpsimd.tensor_tensor(wd_lo[:, j], wd_raw[:], f32(wd_hi[:, j]),
                                        ALU.subtract).then_inc(s_fd_lo[j], 1)

            def act_low(p, j, c):
                n = p * 2 * CH + j * CH + c
                pool.wait_ge(s_at_hi, n + 1)
                nc.gpsimd.tensor_tensor(at_lo[:, j, c * BANK:(c + 1) * BANK], act[:, c % 2],
                                        f32(at_hi[:, j, c * BANK:(c + 1) * BANK]), ALU.subtract).then_inc(s_at_lo, 1)

            def turn(p, last):
                for j in range(2):
                    for c in range(CH):
                        act_low(p, j, c)
                        if c == 0:
                            wd_low(p, j)
                    if not last:
                        wgu_low(p + 1, j)

            wgu_low(0, 0)
            pool.wait_ge(s_mu_hi, 1)
            nc.gpsimd.tensor_tensor(mu_lo[:], mu_raw[:], f32(mu_hi[:]), ALU.subtract).then_inc(s_mu_lo, 1)
            wgu_low(0, 1)
            with pool.Fori(0, PAIRS - 1) as p:
                turn(p, False)
            turn(PAIRS - 1, True)

        @block.scalar
        def _(eng):
            nc.scalar.preload_act_table(ACT.Exp)
            eng.dma_start(gains_raw[:], gains).then_inc(s_gains, 16)
            eng.dma_start(inv_raw[:], inv_map).then_inc(s_small, 16)
            eng.dma_start(gate_raw[:], gate_t).then_inc(s_gate_in, 16)
            eng.wait_ge(s_gains, 16)
            nc.scalar.activation(gain[:], gains_raw[:], ACT.Tanh).then_inc(s_gain, 1)

            def weight_hi(m):
                eng.wait_ge(s_win[m], 16)
                nc.scalar.copy(w_hi(m), w_raw_of(m)).then_inc(s_w_hi, 1)

            def hi_of(ready, done, value, dst, src):
                eng.wait_ge(ready, value)
                nc.scalar.copy(dst, src).then_inc(done, 1)

            def norm_hi(b):
                for j in range(2):
                    hi_of(s_xnt, s_xnt_hi, 2 * b + j + 1, xnt_hi[:, 2 * j:2 * j + 2, :], bank[2 + j][:])

            def out_hi(b):
                for j in range(2):
                    hi_of(s_o, s_o_hi, 2 * b + j + 1, ot_hi[:, 2 * j:2 * j + 2, :], bank[4 + j][:])

            def logits_copy(r):
                eng.wait_ge(s_logit_t, r + 1)
                nc.scalar.copy(logit_t[:], bank[6][0:E, 0:S]).then_inc(s_logit_sb, 1)

            def token_exp(r):
                eng.wait_ge(s_centre, r + 1)
                nc.scalar.activation(prob[:], prob[:], ACT.Exp).then_inc(s_exp_tok, 1)

            def weights_copy(r):
                eng.wait_ge(s_wet, r + 1)
                nc.scalar.copy(we_t[:], bank[6][0:E, 0:S]).then_inc(s_wet_sb, 1)

            def soft_exp(r):
                soft_half = soft.rearrange("p t (h e) -> p t h e", h=2)
                eng.wait_ge(s_gcentre, r + 1)
                nc.scalar.activation(soft, soft, ACT.Exp).then_inc(s_exp_grp, 1)
                eng.wait_ge(s_soft, r + 1)
                nc.scalar.copy(stack_tok[:, :, :, 0:HALF_E], soft_half).then_inc(s_soft_hi, 1)
                nc.scalar.copy(stack_tok[:, :, :, 2 * HALF_E:SOFT_ROWS], soft_half).then_inc(s_stack, 1)

            def soft_t_copy(r):
                eng.wait_ge(s_st, r + 1)
                nc.scalar.copy(soft_t[:, :, bass.ds(r * S, S)],
                               bank[7][0:STACK, :].rearrange("p (h n) -> p h n", h=2)).then_inc(s_st_sb, 1)

            def iteration(b, part):
                r = b - 2
                if part.front:
                    for j in range(2):
                        hi_of(s_q, s_q_hi, 2 * b + j + 1, qt_hi[:, 2 * j:2 * j + 2, :], bank[j][:])
                def key_hi(j):
                    hi_of(s_k, s_k_hi, 2 * b + j + 1, kt_hi[:, 2 * j:2 * j + 2, S:KEYS], bank[2 + j][:])

                if part.front:
                    key_hi(0)
                if part.route:
                    for j in range(2):
                        hi_of(s_x2, s_x2_hi, 2 * r + j + 1, ot_hi[:, 2 * j:2 * j + 2, :], bank[4 + j][:])
                if part.front:
                    key_hi(1)
                    eng.wait_ge(s_ctxt_in, 16 * (b + 1))
                    nc.scalar.copy(kt_hi[:, :, 0:S], ctxt_raw[:]).then_inc(s_kc_hi, 1)
                if part.stack:
                    soft_exp(b - 3)
                if part.route:
                    logits_copy(r)
                if part.back:
                    out_hi(b - 1)
                if part.stack:
                    soft_t_copy(b - 3)
                if part.front:
                    eng.wait_ge(s_ctx_in, 16 * (b + 1))
                    nc.scalar.copy(v_hi[:, 0:ST, :], ctx_raw[:]).then_inc(s_vc_hi, 1)
                if part.route:
                    token_exp(r)
                if part.front:
                    for t in range(ST):
                        hi_of(s_v, s_v_hi, 2 * b + t + 1, v_hi[:, ST + t, :], bank[6 + t][:])
                    if part.first:
                        weight_hi(3)
                        eng.wait_ge(s_w_lo, 4)
                        eng.wait_ge(s_gate_lo, 1)
                    for t in range(ST):
                        eng.wait_ge(s_bias, 2 * b + t + 1)
                        nc.scalar.activation(probs[:, t, :], bank[t][:], ACT.Exp, bias=exp_bias[:, t:t + 1],
                                             scale=SCALE, accum_out=row_sum[:, t:t + 1]).then_inc(s_exp, 1)
                if part.route:
                    weights_copy(r)
                if part.next:
                    norm_hi(b + 1)
                if part.front:
                    for j in range(2):
                        hi_of(s_pt, s_pt_hi, 2 * b + j + 1, pt_hi[:, 2 * j:2 * j + 2, :], bank[6 + j][:])

            weight_hi(0)
            norm_hi(0)
            weight_hi(1)
            weight_hi(2)
            eng.wait_ge(s_gate_in, 16)
            nc.scalar.copy(gate_hi[:], gate_raw[:]).then_inc(s_gate_hi, 1)
            for b in range(LOOP[0]):
                iteration(b, Parts(b))
            with eng.Fori(*LOOP) as b:
                iteration(b, Parts())
            iteration(B - 1, Parts(B - 1))

            def wgu_high(p, j):
                eng.wait_ge(s_fw_in[j], 16 * (p + 1))
                nc.scalar.copy(wgu_hi[:, j], wgu_raw[:]).then_inc(s_fw_hi[j], 1)

            def second_hi(r):
                for j in range(2):
                    hi_of(s_x2, s_x2_hi, 2 * r + j + 1, x2t_hi[:, 2 * j:2 * j + 2, r * S:(r + 1) * S], bank[2 + j][:])

            def normed_again(c):
                eng.wait_ge(s_mv, 2 * c + 2)
                if c >= 2:
                    eng.wait_ge(s_x2t, DT * (c - 1))
                for t in range(4 * c, 4 * c + 4):
                    nc.scalar.activation(xn2[:, t % RING, :], xres[:, t, :], ACT.Identity, bias=mean_rstd[:, t:t + 1],
                                         scale=rstd[:, t:t + 1]).then_inc(s_xf, 1)

            def x2t_high(c):
                for h in range(DT):
                    hi_of(s_x2t, s_x2t_hi, DT * c + h + 1, x2t_hi[:, h, c * BANK:(c + 1) * BANK], bank[h % 2][:])

            eng.wait_ge(s_exp, NT)
            normed_again(0)
            out_hi(B - 1)
            second_hi(B - 2)
            soft_exp(B - 3)
            x2t_high(0)
            soft_t_copy(B - 3)
            logits_copy(B - 2)
            normed_again(1)
            token_exp(B - 2)
            x2t_high(1)
            normed_again(2)
            wgu_high(0, 0)
            weights_copy(B - 2)
            second_hi(B - 1)
            x2t_high(2)
            logits_copy(B - 1)
            token_exp(B - 1)
            eng.wait_ge(s_mu, 16)
            eng.wait_ge(s_y, NT)
            nc.scalar.copy(mu_hi[:], mu_raw[:]).then_inc(s_mu_hi, 1)
            weights_copy(B - 1)
            soft_exp(B - 2)
            soft_t_copy(B - 2)
            wgu_high(0, 1)
            soft_exp(B - 1)
            soft_t_copy(B - 1)
            nc.scalar.preload_act_table(ACT.Silu)

            def scalars_copy(i):
                c, j = i // 2, i % 2
                eng.wait_ge(s_bc, i + 1)
                nc.scalar.copy(scalars[:, j, c * BANK:(c + 1) * BANK], bank[4 + j][:]).then_inc(s_bc_sb, 1)

            for i in range(2 * CH):
                scalars_copy(i)

            def chunk(p, j, c):
                n = p * 2 * CH + j * CH + c
                eng.wait_ge(s_gate, n + 1)
                if j == 1 or c >= 2:
                    eng.wait_ge(s_at_lo, n - 1)
                nc.scalar.activation(act[:, c % 2], bank[2 * (c % 2)][:], ACT.Silu).then_inc(s_silu, 1)
                eng.wait_ge(s_act, n + 1)
                nc.scalar.copy(at_hi[:, j, c * BANK:(c + 1) * BANK], act[:, c % 2]).then_inc(s_at_hi, 1)

            def turn(p, last):
                for j in range(2):
                    for c in range(CH):
                        chunk(p, j, c)
                        if c == 0:
                            eng.wait_ge(s_fd_in[j], 16 * (p + 1))
                            nc.scalar.copy(wd_hi[:, j], wd_raw[:]).then_inc(s_fd_hi[j], 1)
                    if not last:
                        wgu_high(p + 1, j)

            with eng.Fori(0, PAIRS - 1) as p:
                turn(p, False)
            turn(PAIRS - 1, True)

        @block.vector
        def _(dve):
            norm_steps = [0]

            def apart():
                nc.vector.tensor_copy(scrap[:], ident[:, 0:1])

            def step(ins):
                norm_steps[0] += 1
                ins.then_inc(s_norm, 1)
                dve.wait_ge(s_norm, norm_steps[0])

            def rsqrt_of_variance(step, variance, y, width):
                v, z, bits = var_eps[:, 0:width], newton[:, 0:width], seed[:, 0:width]
                step(nc.vector.tensor_scalar(v, variance, EPS, None, ALU.add))
                step(nc.vector.tensor_scalar(bits, v.bitcast(I32), 1, None, ALU.logical_shift_right))
                step(nc.vector.tensor_scalar(bits, bits, -1.0, RSQRT_SEED, ALU.mult, ALU.add))
                step(nc.vector.tensor_copy(y, bits.bitcast(F32)))
                for _ in range(NEWTON):
                    step(nc.vector.tensor_tensor(z, y, y, ALU.mult))
                    step(nc.vector.scalar_tensor_tensor(out=z, in0=z, scalar=-0.5, in1=v, op0=ALU.mult, op1=ALU.mult))
                    step(nc.vector.scalar_tensor_tensor(out=y, in0=z, scalar=1.5, in1=y, op0=ALU.add, op1=ALU.mult))

            def norm_stats(t0, t1):
                for t in range(t0, t1):
                    last = nc.vector.bn_stats(stats_x[:, t, :], xres[:, t, :])
                step(last)
                for t in range(t0, t1):
                    last = nc.vector.bn_aggr(mv[:, t, :], stats_x[:, t, :])
                step(last)
                rsqrt_of_variance(step, mv[:, t0:t1, 1], rstd[:, t0:t1], t1 - t0)

            def norm_apply(b):
                for t in range(ST):
                    n = ST * b + t
                    nc.vector.tensor_scalar(xn[:, t, :], xres[:, bass.ds(n, 1), :], mv[:, bass.ds(n, 1), 0],
                                            rstd[:, bass.ds(n, 1)], ALU.subtract, ALU.mult).then_inc(s_xn, 1)

            def lo_of(hi_done, done, value, dst, src, hi):
                dve.wait_ge(hi_done, value)
                nc.vector.tensor_tensor(dst, src, f32(hi), ALU.subtract).then_inc(done, 1)

            def norm_lo(b):
                for j in range(2):
                    at = slice(2 * j, 2 * j + 2)
                    lo_of(s_xnt_hi, s_xnt_lo, 2 * b + j + 1, xnt_lo[:, at, :], bank[2 + j][:], xnt_hi[:, at, :])

            def out_lo(b):
                for j in range(2):
                    at = slice(2 * j, 2 * j + 2)
                    lo_of(s_o_hi, s_o_lo, 2 * b + j + 1, ot_lo[:, at, :], bank[4 + j][:], ot_hi[:, at, :])

            def weight_lo(m):
                lo_of(s_w_hi, s_w_lo, m + 1, w_lo(m), w_raw_of(m), w_hi(m))

            def residual(b, t):
                n = ST * b + t
                row = xres[:, bass.ds(n, 1), :]
                dve.wait_ge(s_y, n + 1)
                nc.vector.scalar_tensor_tensor(out=row, in0=bank[4 + t][:], scalar=out_coef[:, t:t + 1], in1=row,
                                               op0=ALU.mult, op1=ALU.add).then_inc(s_x1, 1)
                dve.wait_ge(s_x1, n + 1)
                apart()
                nc.vector.bn_stats(stats_2[:, t, :], row).then_inc(s_stat, 1)

            norm2_step = Steps(dve, s_norm2, NORM_STEPS)
            route_step = [Steps(dve, s_route[i], ROUTE_STEPS[i]) for i in range(3)]

            def norm2(r):
                dve.wait_ge(s_stat, ST * (r + 1))
                norm2_step.begin(r)
                apart()
                for t in range(ST):
                    last = nc.vector.bn_aggr(mv_2[:, t, :], stats_2[:, t, :])
                norm2_step(last)
                rsqrt_of_variance(norm2_step, mv_2[:, :, 1], rstd_2[:], ST)
                norm2_step.end()
                for t in range(ST):
                    n = ST * r + t
                    nc.vector.tensor_scalar(xn[:, t, :], xres[:, bass.ds(n, 1), :], mv_2[:, t, 0:1], rstd_2[:, t:t + 1],
                                            ALU.subtract, ALU.mult).then_inc(s_xn2, 1)
                nc.vector.scalar_tensor_tensor(out=mean_rstd[:, bass.ds(ST * r, ST)], in0=mv_2[:, :, 0], scalar=-1.0,
                                               in1=rstd_2[:], op0=ALU.mult, op1=ALU.mult)
                nc.vector.tensor_copy(rstd[:, bass.ds(ST * r, ST)], rstd_2[:]).then_inc(s_mv, 1)

            def per_row(v, n):
                return v.unsqueeze(2).broadcast_to([P, v.shape[1], n])

            def route_centre(r, logits_bank):
                route = route_step[0]
                route.begin(r)
                logits = bank[logits_bank][:, 0:ST * E].rearrange("p (t e) -> p t e", e=E)
                dve.wait_ge(s_logit, r + 1)
                route(nc.vector.tensor_reduce(tok_max[:], logits, AX.X, ALU.max))
                route.end()
                nc.vector.tensor_tensor(prob[:], logits, per_row(tok_max[:], E), ALU.subtract).then_inc(s_centre, 1)

            def route_top(r):
                route = route_step[1]
                route.begin(r)
                dve.wait_ge(s_exp_tok, r + 1)
                route(nc.vector.tensor_reduce(tok_sum[:], prob[:], AX.X, ALU.add))
                route(nc.vector.reciprocal(tok_inv[:], tok_sum[:]))
                route(nc.vector.tensor_tensor(prob[:], prob[:], per_row(tok_inv[:], E), ALU.mult))
                apart()
                for t in range(ST):
                    last = nc.vector.max(top8[:, t, :], prob[:, t, :])
                route(last)
                apart()
                for t in range(ST):
                    last = nc.vector.match_replace(rest[:, t, :], top8[:, t, :], prob[:, t, :], 0.0)
                route(last)
                route.end()
                nc.vector.tensor_tensor(rest[:], prob[:], rest[:], ALU.subtract).then_inc(s_we, 1)

            def route_flat(r):
                dve.wait_ge(s_flat, r + 1)
                nc.vector.tensor_copy(flat, bank[7][:, 0:ST * E].rearrange("p (t e) -> p t e", e=E)).then_inc(s_flat_sb, 1)

            def route_soft(r):
                by_group = flat.rearrange("p t (g s) -> p (t g) s", s=GS)
                soft_group = soft.rearrange("p t (g s) -> p (t g) s", s=GS)
                scal_flat = scal[:].rearrange("p t h g -> p (t h g)")
                scal_hi = stack_tok[:, :, :, SOFT_ROWS:SOFT_ROWS + HALF_G]
                dve.wait_ge(s_flat_sb, r + 1)
                route = route_step[2]
                route.begin(r)
                route(nc.vector.tensor_scalar(soft, flat, 0.0, NEG_INF, ALU.is_equal, ALU.mult))
                route(nc.vector.tensor_tensor(soft, soft, flat, ALU.add))
                route(nc.vector.tensor_reduce(grp_max[:], soft_group, AX.X, ALU.max))
                nc.vector.tensor_tensor(soft_group, soft_group, per_row(grp_max[:], GS),
                                        ALU.subtract).then_inc(s_gcentre, 1)
                route(nc.vector.tensor_reduce(scal_flat, by_group, AX.X, ALU.add))
                route(nc.vector.tensor_scalar(scal_flat, scal_flat, gain[:, 1:2], None, ALU.mult))
                route(nc.vector.tensor_copy(scal_hi, scal[:]))
                route(nc.vector.tensor_tensor(stack_tok[:, :, :, SOFT_ROWS + HALF_G:STACK], scal[:], f32(scal_hi),
                                              ALU.subtract))
                dve.wait_ge(s_exp_grp, r + 1)
                route(nc.vector.tensor_reduce(grp_sum[:], soft_group, AX.X, ALU.add))
                route(nc.vector.reciprocal(grp_inv[:], grp_sum[:]))
                route.end()
                nc.vector.tensor_tensor(soft_group, soft_group, per_row(grp_inv[:], GS),
                                        ALU.mult).then_inc(s_soft, 1)
                dve.wait_ge(s_soft_hi, r + 1)
                nc.vector.tensor_tensor(stack_tok[:, :, :, HALF_E:2 * HALF_E],
                                        soft.rearrange("p t (h e) -> p t h e", h=2),
                                        f32(stack_tok[:, :, :, 0:HALF_E]), ALU.subtract).then_inc(s_stack, 1)

            def coefficient(b):
                dve.wait_ge(s_exp, 2 * b + 2)
                nc.vector.reciprocal(row_inv[:], row_sum[:]).then_inc(s_rinv, 1)
                dve.wait_ge(s_rinv, b + 1)
                nc.vector.tensor_scalar(out_coef[:], row_inv[:], gain[:, 0:1], None, ALU.mult).then_inc(s_coef, 1)

            def iteration(b, part):
                r = b - 2
                if part.front:
                    for j in range(2):
                        at = slice(2 * j, 2 * j + 2)
                        lo_of(s_q_hi, s_q_lo, 2 * b + j + 1, qt_lo[:, at, :], bank[j][:], qt_hi[:, at, :])
                def key_lo(j):
                    at = slice(2 * j, 2 * j + 2)
                    lo_of(s_k_hi, s_k_lo, 2 * b + j + 1, kt_lo[:, at, S:KEYS], bank[2 + j][:], kt_hi[:, at, S:KEYS])

                if part.front:
                    key_lo(0)
                if part.route:
                    for j in range(2):
                        at = slice(2 * j, 2 * j + 2)
                        lo_of(s_x2_hi, s_x2_lo, 2 * r + j + 1, ot_lo[:, at, :], bank[4 + j][:], ot_hi[:, at, :])
                if part.front:
                    key_lo(1)
                if part.first:
                    dve.wait_ge(s_xr, 16)
                    norm_stats(ST, 2 * ST)
                if part.stack:
                    route_soft(b - 3)
                if part.next:
                    norm_apply(b + 1)
                if part.back:
                    out_lo(b - 1)
                if part.route:
                    route_centre(r, 0)
                if part.front:
                    for t in range(ST):
                        lo_of(s_v_hi, s_v_lo, 2 * b + t + 1, v_lo[:, ST + t, :], bank[6 + t][:], v_hi[:, ST + t, :])
                if part.first:
                    weight_lo(3)
                if part.route:
                    route_top(r)
                if part.front:
                    for t in range(ST):
                        dve.wait_ge(s_scores, 2 * b + t + 1)
                        nc.vector.tensor_reduce(neg_max[:, t:t + 1], bank[t][:], AX.X, ALU.max,
                                                negate=True).then_inc(s_max, 1)
                        dve.wait_ge(s_max, 2 * b + t + 1)
                        nc.vector.tensor_scalar(exp_bias[:, t:t + 1], neg_max[:, t:t + 1], SCALE, None,
                                                ALU.mult).then_inc(s_bias, 1)
                if part.next:
                    norm_lo(b + 1)
                if part.back:
                    dve.wait_ge(s_coef, b)
                    residual(b - 1, 0)
                if part.route:
                    route_flat(r)
                if part.back:
                    residual(b - 1, 1)
                    if part.next:
                        norm2(b - 1)
                if part.front:
                    coefficient(b)
                    for j in range(2):
                        at = slice(2 * j, 2 * j + 2)
                        lo_of(s_pt_hi, s_pt_lo, 2 * b + j + 1, pt_lo[:, at, :], bank[6 + j][:], pt_hi[:, at, :])
                if part.back and not part.next:
                    norm2(b - 1)
                if part.first:
                    norm_stats(2 * ST, NT)

            dve.wait_ge(s_x0, 16)
            dve.wait_ge(s_ident, 1)
            norm_stats(0, ST)
            norm_apply(0)
            weight_lo(0)
            norm_lo(0)
            weight_lo(1)
            weight_lo(2)
            dve.wait_ge(s_const, 4)
            step(nc.vector.tensor_scalar(row_group_i[0:SOFT_ROWS], row_i[0:SOFT_ROWS], HALF_E - 1, 3,
                                         ALU.bitwise_and, ALU.logical_shift_right))
            step(nc.vector.tensor_scalar(row_group_i[SOFT_ROWS:STACK], row_i[SOFT_ROWS:STACK], HALF_G - 1, None,
                                         ALU.bitwise_and))
            step(nc.vector.tensor_copy(row_group[:], row_group_i[:]))
            step(nc.vector.tensor_scalar(group_mask[:], col_group[:], row_group[:, 0:1], None, ALU.is_equal))
            dve.wait_ge(s_small, 16)
            step(nc.vector.tensor_copy(inv_f[:], inv_raw[:]))
            step(nc.vector.tensor_scalar(inv_neg[:], inv_f[:], 0.0, float(E), ALU.is_lt, ALU.mult))
            step(nc.vector.tensor_tensor(inv_f[:], inv_f[:], inv_neg[:], ALU.add))
            step(nc.vector.tensor_copy(expert_f[:], expert_i[:]))
            step(nc.vector.tensor_scalar(pick[:], inv_f[:], expert_f[:, 0:1], None, ALU.is_equal))
            dve.wait_ge(s_gain, 1)
            for b in range(LOOP[0]):
                iteration(b, Parts(b))
            with dve.Fori(*LOOP) as b:
                iteration(b, Parts())
            iteration(B - 1, Parts(B - 1))

            def second_lo(r):
                for j in range(2):
                    at, tokens = slice(2 * j, 2 * j + 2), slice(r * S, (r + 1) * S)
                    lo_of(s_x2_hi, s_x2_lo, 2 * r + j + 1, x2t_lo[:, at, tokens], bank[2 + j][:], x2t_hi[:, at, tokens])

            def x2t_low(c):
                at = slice(c * BANK, (c + 1) * BANK)
                for h in range(DT):
                    lo_of(s_x2t_hi, s_x2t_lo, DT * c + h + 1, x2t_lo[:, h, at], bank[h % 2][:], x2t_hi[:, h, at])

            route_soft(B - 3)
            out_lo(B - 1)
            second_lo(B - 2)
            x2t_low(0)
            dve.wait_ge(s_coef, B)
            for t in range(ST):
                residual(B - 1, t)
            route_centre(B - 2, 7)
            norm2(B - 1)
            route_top(B - 2)
            x2t_low(1)
            route_flat(B - 2)
            second_lo(B - 1)
            x2t_low(2)
            route_centre(B - 1, 0)
            route_top(B - 1)
            dve.wait_ge(s_st, B - 2)
            route_soft(B - 2)
            nc.vector.memset(f32(pick_group[:]), 0.0).then_inc(s_pick, 1)
            dve.wait_ge(s_pick, 1)
            nc.vector.tensor_copy(pick_group[SOFT_ROWS:STACK, :], group_mask[SOFT_ROWS:STACK, :]).then_inc(s_pick, 1)
            route_flat(B - 1)
            dve.wait_ge(s_st, B - 1)
            route_soft(B - 1)

            def a_tile(p, j):
                k = 2 * p + j + 1
                columns = group_mask[0:SOFT_ROWS, :].unsqueeze(1).broadcast_to([SOFT_ROWS, 2, P])
                dve.wait_ge(s_a, k)
                nc.vector.tensor_tensor(a_tmp[:], bank[4 + j][0:SOFT_ROWS, 0:2 * P].rearrange("p (m r) -> p m r", m=2),
                                        columns, ALU.mult).then_inc(s_a_masked, 1)
                dve.wait_ge(s_a_masked, k)
                nc.vector.tensor_copy(a_stack[:, j], a_tmp[:]).then_inc(s_a_hi, 1)
                dve.wait_ge(s_a_hi, k)
                low = slice(2 * HALF_E, SOFT_ROWS)
                nc.vector.tensor_tensor(a_stack[low, j], a_tmp[low], f32(a_stack[low, j]),
                                        ALU.subtract).then_inc(s_a_st, 1)

            def chunk(p, j, c):
                n = p * 2 * CH + j * CH + c
                s = c % 2
                dve.wait_ge(s_silu, n + 1)
                dve.wait_ge(s_up, n + 1)
                nc.vector.tensor_tensor(act[:, s], act[:, s], bank[2 * s + 1][:], ALU.mult).then_inc(s_prod, 1)
                dve.wait_ge(s_prod, n + 1)
                nc.vector.tensor_tensor(act[:, s], act[:, s], scalars[:, j, c * BANK:(c + 1) * BANK],
                                        ALU.mult).then_inc(s_act, 1)

            def turn(p, last):
                for j in range(2):
                    a_tile(p, j)
                    for c in range(CH):
                        chunk(p, j, c)
                for t in range(NT):
                    dve.wait_ge(s_down, NT * p + t + 1)
                    nc.vector.tensor_tensor(xres[:, t, :], xres[:, t, :], bank[6 + t % 2][:], ALU.add).then_inc(s_res, 1)

            dve.wait_ge(s_bc_sb, 2 * CH)
            with dve.Fori(0, PAIRS - 1) as p:
                turn(p, False)
            turn(PAIRS - 1, True)

        @block.tensor
        def _(pe):
            def mm(out_ap, pairs):
                return accumulate(nc, out_ap, pairs)

            def project_t(m, b0, ready, j):
                for e in (2 * j, 2 * j + 1):
                    last = mm(bank[b0 + e // 2][:, (e % 2) * S:(e % 2 + 1) * S],
                              split_products(lambda k: w_hi(m)[:, k, e * P:(e + 1) * P], lambda k: w_lo(m)[:, k, e * P:(e + 1) * P],
                                             lambda k: xnt_hi[:, k, :], lambda k: xnt_lo[:, k, :], range(DT)))
                    if e % 2:
                        last.then_inc(ready, 1)

            def transposes(src, b0, ready):
                for h in range(DT):
                    for t in range(ST):
                        last = nc.tensor.transpose(bank[b0 + h // 2][:, (h % 2) * S + t * P:(h % 2) * S + (t + 1) * P],
                                                   src[:, t, h * P:(h + 1) * P], ident[:])
                    if h % 2:
                        last.then_inc(ready, 1)

            def norm_transposes(b):
                pe.wait_ge(s_xn, 2 * b + 2)
                transposes(xn, 2, s_xnt)

            def attend(b):
                pe.wait_ge(s_pt_lo, 2 * b + 2)
                pe.wait_ge(s_v_lo, 2 * b + 2)
                pe.wait_ge(s_vc_lo, b + 1)
                for d in range(DT):
                    at = slice(d * P, (d + 1) * P)
                    last = mm(bank[4 + d // 2][:, (d % 2) * S:(d % 2 + 1) * S],
                              split_products(lambda k: v_hi[:, k, at], lambda k: v_lo[:, k, at],
                                             lambda k: pt_hi[:, k, :], lambda k: pt_lo[:, k, :], range(KT)))
                    if d % 2:
                        last.then_inc(s_o, 1)

            def output(b, t):
                at = slice(t * P, (t + 1) * P)
                mm(bank[4 + t][:], split_products(lambda k: ot_hi[:, k, at], lambda k: ot_lo[:, k, at],
                                                  lambda k: w_hi(3)[:, k, :], lambda k: w_lo(3)[:, k, :],
                                                  range(DT))).then_inc(s_y, 1)

            def values(t):
                at = slice(t * P, (t + 1) * P)
                mm(bank[6 + t][:], split_products(lambda k: xnt_hi[:, k, at], lambda k: xnt_lo[:, k, at],
                                                  lambda k: w_hi(2)[:, k, :], lambda k: w_lo(2)[:, k, :],
                                                  range(DT))).then_inc(s_v, 1)

            def stack_transposes(r):
                pe.wait_ge(s_stack, 2 * r + 2)
                for h in range(2):
                    for t in range(ST):
                        last = nc.tensor.transpose(bank[7][0:STACK, h * S + t * P:h * S + (t + 1) * P],
                                                   f32(stack_tok[:, t, h, :]), ident[:])
                last.then_inc(s_st, 1)

            def logits(r, hi, lo):
                pe.wait_ge(s_x2_lo, 2 * r + 2)
                pe.wait_ge(s_gate_lo, 1)
                mm(bank[6][0:E, 0:S], split_products(lambda k: gate_hi[:, k, :], lambda k: gate_lo[:, k, :], hi, lo,
                                                     range(DT))).then_inc(s_logit_t, 1)

            def logit_transposes(logits_bank):
                for t in range(ST):
                    last = nc.tensor.transpose(bank[logits_bank][:, t * E:(t + 1) * E], logit_t[:, t * P:(t + 1) * P],
                                               ident[0:E, 0:E])
                last.then_inc(s_logit, 1)

            def weight_transposes():
                for t in range(ST):
                    last = nc.tensor.transpose(bank[6][0:E, t * P:(t + 1) * P], rest[:, t, :], ident[:])
                last.then_inc(s_wet, 1)

            def flat_products():
                for t in range(ST):
                    last = nc.tensor.matmul(bank[7][:, t * E:(t + 1) * E], we_t[:, t * P:(t + 1) * P], pick[:],
                                            start=True, stop=True)
                last.then_inc(s_flat, 1)

            def iteration(b, part):
                r = b - 2
                pe.wait_ge(s_xnt_lo, 2 * b + 2)
                if part.first:
                    pe.wait_ge(s_w_lo, 1)
                else:
                    pe.wait_ge(s_exp, 2 * b)
                for j in range(2):
                    project_t(0, 0, s_q, j)
                if part.first:
                    pe.wait_ge(s_w_lo, 2)
                project_t(1, 2, s_k, 0)
                if part.route:
                    pe.wait_ge(s_xn2, 2 * r + 2)
                    transposes(xn, 4, s_x2)
                project_t(1, 2, s_k, 1)
                if part.route:
                    pe.wait_ge(s_pt_lo, 2 * b)
                    logits(r, lambda k: ot_hi[:, k, :], lambda k: ot_lo[:, k, :])
                if part.back:
                    attend(b - 1)
                if part.stack:
                    stack_transposes(b - 3)
                if part.route:
                    pe.wait_ge(s_logit_sb, r + 1)
                    pe.wait_ge(s_q_lo, 2 * b + 2)
                if part.first:
                    pe.wait_ge(s_w_lo, 3)
                else:
                    pe.wait_ge(s_pt_lo, 2 * b)
                values(0)
                if part.route:
                    logit_transposes(0)
                if part.stack:
                    pe.wait_ge(s_st_sb, b - 2)
                values(1)
                pe.wait_ge(s_q_lo, 2 * b + 2)
                pe.wait_ge(s_k_lo, 2 * b + 2)
                pe.wait_ge(s_kc_lo, b + 1)
                if part.route:
                    pe.wait_ge(s_centre, r + 1)
                for t in range(ST):
                    at = slice(t * P, (t + 1) * P)
                    mm(bank[t][:], split_products(lambda k: qt_hi[:, k, at], lambda k: qt_lo[:, k, at],
                                                  lambda k: kt_hi[:, k, :], lambda k: kt_lo[:, k, :],
                                                  range(DT))).then_inc(s_scores, 1)
                if part.route:
                    pe.wait_ge(s_v_lo, 2 * b + 1)
                    pe.wait_ge(s_we, r + 1)
                    if part.next:
                        norm_transposes(b + 1)
                    weight_transposes()
                elif part.next:
                    norm_transposes(b + 1)
                if part.back:
                    pe.wait_ge(s_o_lo, 2 * b)
                    pe.wait_ge(s_w_lo, 4)
                    output(b - 1, 0)
                if part.route:
                    pe.wait_ge(s_wet_sb, r + 1)
                    pe.wait_ge(s_v_lo, 2 * b + 2)
                    flat_products()
                if part.back:
                    output(b - 1, 1)
                pe.wait_ge(s_exp, 2 * b + 2)
                pe.wait_ge(s_v_lo, 2 * b + 2)
                if part.route:
                    pe.wait_ge(s_flat_sb, r + 1)
                transposes(probs, 6, s_pt)

            pe.wait_ge(s_ident, 1)
            norm_transposes(0)
            for b in range(LOOP[0]):
                iteration(b, Parts(b))
            with pe.Fori(*LOOP) as b:
                iteration(b, Parts())
            iteration(B - 1, Parts(B - 1))

            def second_transposes(r):
                pe.wait_ge(s_xn2, 2 * r + 2)
                transposes(xn, 2, s_x2)

            def second_tokens(r):
                tokens = slice(r * S, (r + 1) * S)
                return lambda k: x2t_hi[:, k, tokens], lambda k: x2t_lo[:, k, tokens]

            def x2t_transposes(c):
                pe.wait_ge(s_xf, 4 * c + 4)
                for h in range(DT):
                    m = DT * c + h
                    if m >= 2:
                        pe.wait_ge(s_x2t_lo, m - 1)
                    for t in range(4):
                        last = nc.tensor.transpose(bank[h % 2][:, t * P:(t + 1) * P],
                                                   xn2[:, (4 * c + t) % RING, h * P:(h + 1) * P], ident[:])
                    last.then_inc(s_x2t, 1)

            attend(B - 1)
            second_transposes(B - 2)
            x2t_transposes(0)
            stack_transposes(B - 3)
            logits(B - 2, *second_tokens(B - 2))
            pe.wait_ge(s_o_lo, NT)
            for t in range(ST):
                output(B - 1, t)
            pe.wait_ge(s_logit_sb, B - 1)
            pe.wait_ge(s_st_sb, B - 2)
            logit_transposes(7)
            x2t_transposes(1)
            pe.wait_ge(s_we, B - 1)
            weight_transposes()
            pe.wait_ge(s_wet_sb, B - 1)
            flat_products()
            pe.wait_ge(s_x2_lo, NT - 2)
            second_transposes(B - 1)
            x2t_transposes(2)
            logits(B - 1, *second_tokens(B - 1))
            pe.wait_ge(s_logit_sb, B)
            pe.wait_ge(s_x2t_lo, DT * (CH - 1))
            logit_transposes(0)
            pe.wait_ge(s_we, B)
            weight_transposes()
            pe.wait_ge(s_wet_sb, B)
            pe.wait_ge(s_flat_sb, B - 1)
            flat_products()
            pe.wait_ge(s_flat_sb, B)
            stack_transposes(B - 2)
            pe.wait_ge(s_st_sb, B - 1)
            stack_transposes(B - 1)
            pe.wait_ge(s_pick, 2)
            pe.wait_ge(s_st_sb, B)
            pe.wait_ge(s_x1, NT)
            for i in range(2 * CH):
                if i >= 2:
                    pe.wait_ge(s_bc_sb, i - 1)
                nc.tensor.matmul(bank[4 + i % 2][:], pick_group[:], soft_t[:, i % 2, i // 2 * BANK:(i // 2 + 1) * BANK],
                                 start=True, stop=True).then_inc(s_bc, 1)
            pe.wait_ge(s_bc_sb, 2 * CH)
            pe.wait_ge(s_mu_lo, 1)

            def a_products(p, j):
                mm(bank[4 + j][0:SOFT_ROWS, 0:2 * P],
                   split_products(lambda k: mu_hi[:, k, j, :], lambda k: mu_lo[:, k, j, :],
                                  lambda k: wgu_hi[:, j, k, :], lambda k: wgu_lo[:, j, k, :],
                                  range(DT))).then_inc(s_a, 1)

            def chunk(p, j, c):
                n = p * 2 * CH + j * CH + c
                at = slice(c * BANK, (c + 1) * BANK)
                b0 = 2 * (c % 2)
                if j == 1 or c >= 2:
                    pe.wait_ge(s_prod, n - 1)
                if c == 0:
                    pe.wait_ge(s_fw_lo[j], p + 1)
                for m in range(2):
                    rows = slice(m * P, (m + 1) * P)
                    pairs = split_products(lambda k: wgu_hi[:, j, k, rows], lambda k: wgu_lo[:, j, k, rows],
                                           lambda k: x2t_hi[:, k, at], lambda k: x2t_lo[:, k, at], range(DT))
                    for q, (stationary, moving) in enumerate(pairs):
                        nc.tensor.matmul(bank[b0 + m][:], stationary, moving, start=q == 0, stop=False)
                    if c == 0 and m == 0:
                        a_products(p, j)
                    if c > 0:
                        soft_product(j, c, m)
                if c == 0:
                    pe.wait_ge(s_a_st, 2 * p + j + 1)
                    for m in range(2):
                        soft_product(j, c, m)

            def soft_product(j, c, m):
                nc.tensor.matmul(bank[2 * (c % 2) + m][:], a_stack[:, j, m, :],
                                 soft_t[0:SOFT_ROWS, j, c * BANK:(c + 1) * BANK], start=False,
                                 stop=True).then_inc((s_gate, s_up)[m], 1)

            def turn(p, last):
                for j in range(2):
                    for c in range(CH):
                        chunk(p, j, c)
                for j in range(2):
                    pe.wait_ge(s_fd_lo[j], p + 1)
                for t in range(NT):
                    pe.wait_ge(s_at_lo, 2 * CH * p + CH + t // 4 + 1)
                    if t >= 2:
                        pe.wait_ge(s_res, NT * p + t - 1)
                    at = slice(t * P, (t + 1) * P)
                    mm(bank[6 + t % 2][:], split_products(lambda k: at_hi[:, k, at], lambda k: at_lo[:, k, at],
                                                          lambda k: wd_hi[:, k, :], lambda k: wd_lo[:, k, :],
                                                          range(2))).then_inc(s_down, 1)

            with pe.Fori(0, PAIRS - 1) as p:
                turn(p, False)
            turn(PAIRS - 1, True)


def kernel(**inputs):
    import numpy as np
    import concourse.bacc as bacc
    from concourse.bass_utils import run_bass_kernel_spmd

    given = {name: np.asarray(value) for name, value in inputs.items()}

    def by_k_tile(w):
        return w.T.reshape(DT, P, w.shape[0]).transpose(1, 0, 2)

    w_qkvo = np.stack([by_k_tile(given[f"L0_xattn_w{n}"]) for n in "qkvo"])
    ctx = given["ctx_2048"]
    ctx_t = ctx.transpose(0, 2, 1).reshape(B, DT, P, S).transpose(0, 2, 1, 3)

    def inner_rows(w):
        return w.reshape(2, HALF_G, PAIRS, SLICE, D).transpose(2, 0, 1, 3, 4).reshape(PAIRS, 2, P, D)

    gate_up = np.stack([inner_rows(given[f"L0_ffn_{n}_proj_w"]) for n in ("gate", "up")], axis=2)
    gate_up = gate_up.reshape(PAIRS, 2, 2, P, DT, P).transpose(0, 1, 5, 4, 2, 3).reshape(PAIRS, 2, P, DT, 2 * P)
    down = inner_rows(given["L0_ffn_down_proj_w"].transpose(0, 2, 1))
    mask_up = given["L0_ffn_mask_up_w"].transpose(1, 0, 2).reshape(DT, P, 2, 1, HALF_E).transpose(1, 0, 2, 3, 4)
    mask_up = np.broadcast_to(mask_up, (P, DT, 2, 3, HALF_E)).reshape(P, DT, 2, SOFT_ROWS)
    arrays = {
        "x": given["x"],
        "ctx": ctx,
        "ctx_t": ctx_t,
        "w_qkvo": w_qkvo,
        "w_gate_up": gate_up,
        "w_down": down,
        "mask_up": mask_up,
        "gate_t": by_k_tile(given["L0_ffn_gate_w"]),
        "inv_map": np.broadcast_to(given["L0_ffn_inv_map"].reshape(1, E), (E, E)),
        "gains": np.broadcast_to(np.concatenate([given["g_xattn"], given["g_ffn"]]), (P, 2)),
    }
    arrays = {f"in_{name}": np.ascontiguousarray(value) for name, value in arrays.items()}
    nc = bacc.Bacc("TRN2", target_bir_lowering=False, num_devices=1)
    args = [nc.dram_tensor(name, value.shape, mybir.dt.from_np(value.dtype), kind="ExternalInput").ap()
            for name, value in arrays.items()]
    out = nc.dram_tensor("out", (B, S, D), F32, kind="ExternalOutput").ap()
    layer_program(nc, *args, out)
    result = run_bass_kernel_spmd(nc, [arrays], core_ids=[0])
    return result.results[0]["out"]
```

```python
from contextlib import ExitStack

import concourse.bass as bass
from concourse import mybir

ALU = mybir.AluOpType
ACT = mybir.ActivationFunctionType
AX = mybir.AxisListType
F32 = mybir.dt.float32
F32R = mybir.dt.float32r
I32 = mybir.dt.int32

P = 128
B, S, D = 8, 256, 512
DT = D // P
ST = S // P
NT = B * ST
N = B * S
KEYS = 2 * S
KT = KEYS // P
BANK = 512
CH = N // BANK
E, G, GS, INNER = 64, 8, 8, 352
HALF_E = E // 2
HALF_G = G // 2
PAIRS = G * INNER // P // 2
X2T_BANK = ((0, 1, 6, 7), (4, 5, 4, 5), (4, 5, 4, 5))
SLICE = P // HALF_G
STACK = 4 * HALF_E
A_HI, A_LO, A_REST, A_HI_2 = (slice(i * HALF_E, (i + 1) * HALF_E) for i in range(4))
SCALE = float(D) ** -0.5
EPS = 1e-5
NEG_INF = -1e9
RSQRT_SEED = float(0x5F3759DF)
NEWTON = 3
NORM_STEPS = 5 + 3 * NEWTON
ROUTE_STEPS = (1, 5, 6)
LOOP = (3, B - 1)
RING = 8


def is_first(p):
    return isinstance(p, int) and p == 0


def f32(ap):
    return ap.bitcast(F32)


def split_products(hi_l, lo_l, hi_r, lo_r, tiles):
    return [pair for k in tiles for pair in
            ((lo_l(k), hi_r(k)), (hi_l(k), lo_r(k)), (hi_l(k), hi_r(k)))]


def accumulate(nc, out, pairs):
    for n, (stationary, moving) in enumerate(pairs):
        last = nc.tensor.matmul(out, stationary, moving, start=n == 0, stop=n == len(pairs) - 1)
    return last


class Steps:

    def __init__(self, engine, semaphore, per_turn):
        self.engine, self.semaphore, self.per_turn = engine, semaphore, per_turn

    def begin(self, turn):
        self.before, self.n = turn * self.per_turn, 0

    def __call__(self, instruction):
        self.n += 1
        instruction.then_inc(self.semaphore, 1)
        self.engine.wait_ge(self.semaphore, self.before + self.n)

    def end(self):
        assert self.n == self.per_turn


class Parts:

    def __init__(self, b=None):
        self.first = b == 0
        self.front = b is None or b < B
        self.next = b is None or b + 1 < B
        self.back = b is None or 1 <= b <= B
        self.route = b is None or 2 <= b <= B + 1
        self.stack = b is None or b >= 3


def layer_program(nc, x, ctx_nat, ctx_t, w_qkvo, w_gate_up, w_down, mask_up, gate_t, inv_map, gains, out):
    with ExitStack() as stack:
        def sem(name):
            return stack.enter_context(nc.semaphore(name))

        def sb(where, name, shape, dt):
            return where.enter_context(nc.sbuf_tensor(name, shape, dt))

        xres = sb(stack, "xres", [P, NT, D], F32)
        ident = sb(stack, "ident", [P, P], F32)
        group_mask = sb(stack, "group_mask", [STACK, P], F32)
        soft_t = sb(stack, "soft_t", [STACK, 2, N], F32R)
        scal_tok = sb(stack, "scal_tok", [P, NT, 2, HALF_G], F32)
        stats_x = sb(stack, "stats_x", [P, NT, 6], F32)
        mv = sb(stack, "mv", [P, NT, 2], F32)
        var_eps = sb(stack, "var_eps", [P, NT], F32)
        newton = sb(stack, "newton", [P, NT], F32)
        rstd = sb(stack, "rstd", [P, NT], F32)
        mean_rstd = sb(stack, "mean_rstd", [P, NT], F32)
        seed = sb(stack, "seed", [P, NT], I32)
        scrap = sb(stack, "scrap", [P, 1], F32)
        stats_2 = sb(stack, "stats_2", [P, ST, 6], F32)
        mv_2 = sb(stack, "mv_2", [P, ST, 2], F32)
        rstd_2 = sb(stack, "rstd_2", [P, ST], F32)
        gains_raw = sb(stack, "gains_raw", [P, 2], F32)
        gain = sb(stack, "gain", [P, 2], F32)
        neg_max = sb(stack, "neg_max", [P, ST], F32)
        exp_bias = sb(stack, "exp_bias", [P, ST], F32)
        row_sum = sb(stack, "row_sum", [P, ST], F32)
        row_inv = sb(stack, "row_inv", [P, ST], F32)
        out_coef = sb(stack, "out_coef", [P, ST], F32)
        row_i = sb(stack, "row_i", [STACK, 1], I32)
        row_group_i = sb(stack, "row_group_i", [STACK, 1], I32)
        row_group = sb(stack, "row_group", [STACK, 1], F32)

        a = ExitStack()
        w_hi_qkv = sb(a, "w_hi_qkv", [P, 3, DT, D], F32R)
        w_lo_qkv = sb(a, "w_lo_qkv", [P, 3, DT, D], F32R)
        xnt_hi = sb(a, "xnt_hi", [P, DT, S], F32R)
        xnt_lo = sb(a, "xnt_lo", [P, DT, S], F32R)
        qt_hi = sb(a, "qt_hi", [P, DT, S], F32R)
        qt_lo = sb(a, "qt_lo", [P, DT, S], F32R)
        kt_hi = sb(a, "kt_hi", [P, DT, KEYS], F32R)
        kt_lo = sb(a, "kt_lo", [P, DT, KEYS], F32R)
        w_hi_o = sb(a, "w_hi_o", [P, DT, D], F32R)
        with ExitStack() as early:
            wv_raw = sb(early, "wv_raw", [P, DT, D], F32)
        w_lo_o = sb(a, "w_lo_o", [P, DT, D], F32R)
        v_hi = sb(a, "v_hi", [P, KT, D], F32R)
        v_lo = sb(a, "v_lo", [P, KT, D], F32R)
        ctxt_raw = sb(a, "ctxt_raw", [P, DT, S], F32)
        ctx_raw = sb(a, "ctx_raw", [P, ST, D], F32)
        gate_w = sb(a, "gate_w", [P, DT, 2, E], F32R)
        fold = sb(a, "fold", [2 * E, E], F32)
        inv_raw = sb(a, "inv_raw", [E, E], I32)
        inv_f = sb(a, "inv_f", [E, E], F32)
        inv_neg = sb(a, "inv_neg", [E, E], F32)
        expert_i = sb(a, "expert_i", [E, 1], I32)
        expert_f = sb(a, "expert_f", [E, 1], F32)
        pick = sb(a, "pick", [E, E], F32)
        with ExitStack() as setup:
            w_raw = sb(setup, "w_raw", [P, 2, DT, D], F32)
            col_group = sb(setup, "col_group", [STACK, P], I32)
            gate_raw = sb(setup, "gate_raw", [P, DT, E], F32)
        pt_hi = sb(a, "pt_hi", [P, KT, S], F32R)
        pt_lo = sb(a, "pt_lo", [P, KT, S], F32R)
        probs = sb(a, "probs", [P, ST, KEYS], F32)
        ot_hi = sb(a, "ot_hi", [P, DT, S], F32R)
        ot_lo = sb(a, "ot_lo", [P, DT, S], F32R)
        prob = sb(a, "prob", [P, ST, E], F32)
        top8 = sb(a, "top8", [P, ST, 8], F32)
        rest = sb(a, "rest", [P, ST, E], F32)
        flat_buf = sb(a, "flat", [P, ST, E], F32)
        soft_buf = sb(a, "soft", [P, ST, E], F32)
        tok_max = sb(a, "tok_max", [P, ST], F32)
        tok_sum = sb(a, "tok_sum", [P, ST], F32)
        tok_inv = sb(a, "tok_inv", [P, ST], F32)
        grp_max = sb(a, "grp_max", [P, ST * G], F32)
        grp_sum = sb(a, "grp_sum", [P, ST * G], F32)
        grp_inv = sb(a, "grp_inv", [P, ST * G], F32)
        scal = sb(a, "scal", [P, ST, 2, HALF_G], F32)
        logit_t = sb(a, "logit_t", [2 * E, S], F32)
        we_t = sb(a, "we_t", [E, S], F32)
        stack_tok = sb(a, "stack_tok", [P, ST, 2, STACK], F32R)
        xn = sb(a, "xn", [P, ST, D], F32)
        a.close()
        flat, soft = flat_buf[:], soft_buf[:]

        f = stack.enter_context(ExitStack())
        x2t_hi = sb(f, "x2t_hi", [P, DT, N], F32R)
        x2t_lo = sb(f, "x2t_lo", [P, DT, N], F32R)
        with ExitStack() as before_scalars:
            xn2 = sb(before_scalars, "xn2", [P, RING, D], F32)
        scalars = sb(f, "scalars", [P, 2, N], F32)
        mu = sb(f, "mu", [P, DT, 2, STACK], F32R)
        wd_hi = sb(f, "wd_hi", [P, 2, D], F32R)
        wd_lo = sb(f, "wd_lo", [P, 2, D], F32R)
        a_stack = sb(f, "a_stack", [STACK, 2, 2, P], F32R)
        a_tmp = sb(f, "a_tmp", [STACK, 2, P], F32)
        sb(f, "wo_rest", [P, 2 * P], F32)
        wgu_hi = sb(f, "wgu_hi", [P, 2, DT, 2 * P], F32R)
        wgu_lo = sb(f, "wgu_lo", [P, 2, DT, 2 * P], F32R)
        wgu_raw = sb(f, "wgu_raw", [P, DT, 2 * P], F32)
        wd_raw = sb(f, "wd_raw", [P, D], F32)
        sb(f, "context_rest", [P, D], F32)
        act = sb(f, "act", [P, 2, BANK], F32)
        with ExitStack() as before_ffn:
            mu_raw = sb(before_ffn, "mu_raw", [P, DT, 2, HALF_E], F32)
            sb(before_ffn, "at_hi_0", [P, N - DT * 2 * HALF_E], F32)
            wide = sb(before_ffn, "wide", [P, 2, 4, 2, P], F32)
        at_hi = sb(f, "at_hi", [P, 2, N], F32R)
        at_lo = sb(f, "at_lo", [P, 2, N], F32R)

        bank = [stack.enter_context(nc.psum_tensor(f"bank{i}", [P, BANK], F32)) for i in range(8)]

        s_x0, s_xr, s_gains, s_small, s_mu = map(sem, ("x0_in", "xr_in", "gains_in", "small_in", "mu_in"))
        s_win = [sem(f"w_in{m}") for m in range(4)]
        s_ctxt_in, s_ctx_in = sem("ctxt_in"), sem("ctx_in")
        s_w_hi, s_w_lo = sem("w_hi_done"), sem("w_lo_done")
        s_gain = sem("gain_ready")
        s_const, s_ident = sem("const_steps"), sem("ident_ready")
        s_gate_hi, s_gate_lo, s_gate_in = sem("gate_w_hi"), sem("gate_w_lo"), sem("gate_w_in")
        s_norm = sem("norm_steps")
        s_xn, s_xnt, s_xnt_hi, s_xnt_lo = map(sem, ("xn_ready", "xnt_ready", "xnt_hi_done", "xnt_lo_done"))
        s_q, s_q_hi, s_q_lo = map(sem, ("q_ready", "q_hi_done", "q_lo_done"))
        s_k, s_k_hi, s_k_lo = map(sem, ("k_ready", "k_hi_done", "k_lo_done"))
        s_v, s_v_hi, s_v_lo = map(sem, ("v_ready", "v_hi_done", "v_lo_done"))
        s_o, s_o_hi, s_o_lo = map(sem, ("o_ready", "o_hi_done", "o_lo_done"))
        s_pt, s_pt_hi, s_pt_lo = map(sem, ("pt_ready", "pt_hi_done", "pt_lo_done"))
        s_kc_hi, s_kc_lo, s_vc_hi, s_vc_lo = map(sem, ("kc_hi", "kc_lo", "vc_hi", "vc_lo"))
        s_scores, s_max, s_bias, s_exp = map(sem, ("scores_ready", "max_ready", "bias_ready", "exp_done"))
        s_rinv, s_coef, s_y, s_x1, s_stat = map(sem, ("row_inv_ready", "coef_ready", "y_ready", "x1_done", "x1_stats"))
        s_norm2, s_xn2, s_mv = map(sem, ("norm2_steps", "xn2_ready", "mv_saved"))
        s_x2, s_x2_hi, s_x2_lo = map(sem, ("x2_ready", "x2_hi_done", "x2_lo_done"))
        s_logit_t, s_logit_sb, s_logit = map(sem, ("logit_t_ready", "logit_t_copied", "logits_ready"))
        s_route = [sem(f"route_steps{i}") for i in range(3)]
        s_centre, s_exp_tok, s_gcentre, s_exp_grp = map(sem, ("centred", "exp_tokens", "group_centred", "exp_groups"))
        s_we, s_wet, s_wet_sb, s_flat = map(sem, ("we_ready", "wet_ready", "wet_copied", "flat_ready"))
        s_flat_sb, s_soft, s_soft_hi, s_stack, s_st, s_st_sb = map(
            sem, ("flat_copied", "soft_ready", "soft_hi_done", "stack_done", "soft_t_ready", "soft_t_copied"))
        s_xf, s_x2t, s_x2t_hi, s_x2t_lo = map(sem, ("ffn_xn_ready", "x2t_ready", "x2t_hi_done", "x2t_lo_done"))
        s_mu_hi, s_mu_lo = sem("mu_hi_done"), sem("mu_lo_done")
        s_fw_in = [sem("wgu_in0"), sem("wgu_in1")]
        s_fd_in = [sem("wd_in0"), sem("wd_in1")]
        s_fw_hi = [sem("wgu_hi0"), sem("wgu_hi1")]
        s_fw_lo = [sem("wgu_lo0"), sem("wgu_lo1")]
        s_fd_hi = [sem("wd_hi0"), sem("wd_hi1")]
        s_fd_lo = [sem("wd_lo0"), sem("wd_lo1")]
        s_a, s_a_masked, s_a_hi, s_a_st = map(sem, ("a_ready", "a_masked", "a_hi", "a_stack_done"))
        s_scal, s_wide = sem("scalars_kept"), sem("scalars_widened")
        s_bc, s_bc_sb = sem("scalars_ready"), sem("scalars_copied")
        s_gate, s_up, s_silu, s_prod, s_act = map(sem, ("gate_ready", "up_ready", "silu_done", "prod_done", "act_ready"))
        s_at_hi, s_at_lo = sem("at_hi_done"), sem("at_lo_done")
        s_down, s_res = sem("down_ready"), sem("residual_done")
        s_out = sem("out_stored")

        x_tiles = x.rearrange("b (t p) d -> p (b t) d", p=P)
        out_tiles = out.rearrange("b (t p) d -> p (b t) d", p=P)
        ctx_tiles = ctx_nat.rearrange("b (t p) d -> b p t d", p=P)

        def w_raw_of(m):
            return wv_raw[:] if m == 2 else w_raw[:, m % 3]

        def w_hi(m):
            return w_hi_o[:] if m == 3 else w_hi_qkv[:, m]

        def w_lo(m):
            return w_lo_o[:] if m == 3 else w_lo_qkv[:, m]

        block = stack.enter_context(nc.Block())

        @block.sync
        def _(sp):
            sp.dma_start(xres[:, 0:ST, :], x_tiles[:, 0:ST, :]).then_inc(s_x0, 16)
            for m in range(2):
                sp.dma_start(w_raw_of(m), w_qkvo[m]).then_inc(s_win[m], 16)
            sp.dma_start(w_raw_of(2), w_qkvo[2]).then_inc(s_win[2], 16)
            sp.dma_start(ctxt_raw[:], ctx_t[0]).then_inc(s_ctxt_in, 16)
            sp.dma_start(ctx_raw[:], ctx_tiles[0]).then_inc(s_ctx_in, 16)
            sp.wait_ge(s_w_lo, 1)
            sp.dma_start(w_raw_of(3), w_qkvo[3]).then_inc(s_win[3], 16)
            sp.dma_start(xres[:, ST:NT, :], x_tiles[:, ST:NT, :]).then_inc(s_xr, 16)
            with sp.Fori(1, B) as b:
                sp.wait_ge(s_kc_lo, b)
                sp.dma_start(ctxt_raw[:], ctx_t[b]).then_inc(s_ctxt_in, 16)
                sp.wait_ge(s_vc_lo, b)
                sp.dma_start(ctx_raw[:], ctx_tiles[b]).then_inc(s_ctx_in, 16)
            sp.wait_ge(s_o, NT)
            sp.dma_start(wgu_raw[:], w_gate_up[0, 0]).then_inc(s_fw_in[0], 16)
            sp.dma_start(mu_raw[:], mask_up).then_inc(s_mu, 16)
            sp.dma_start(wd_raw[:], w_down[0, 0]).then_inc(s_fd_in[0], 16)
            sp.wait_ge(s_fw_lo[0], 1)
            sp.dma_start(wgu_raw[:], w_gate_up[0, 1]).then_inc(s_fw_in[1], 16)
            sp.wait_ge(s_fd_lo[0], 1)
            sp.dma_start(wd_raw[:], w_down[0, 1]).then_inc(s_fd_in[1], 16)
            with sp.Fori(1, PAIRS) as p:
                for j in range(2):
                    sp.wait_ge(s_fw_lo[1 - j], p + j)
                    sp.dma_start(wgu_raw[:], w_gate_up[p, j]).then_inc(s_fw_in[j], 16)
                for j in range(2):
                    sp.wait_ge(s_fd_lo[1 - j], p + j)
                    sp.dma_start(wd_raw[:], w_down[p, j]).then_inc(s_fd_in[j], 16)
            for b in range(B):
                sp.wait_ge(s_res, (PAIRS - 1) * NT + ST * (b + 1))
                sp.dma_start(out_tiles[:, ST * b:ST * (b + 1), :], xres[:, ST * b:ST * (b + 1), :]).then_inc(s_out, 16)
            sp.wait_ge(s_out, 16 * B)

        @block.gpsimd
        def _(pool):
            nc.gpsimd.memset(ident[:], 0.0).then_inc(s_const, 1)
            nc.gpsimd.iota(row_i[:], [[0, 1]], base=0, channel_multiplier=1).then_inc(s_const, 1)
            nc.gpsimd.iota(expert_i[:], [[0, 1]], base=0, channel_multiplier=1).then_inc(s_const, 1)
            nc.gpsimd.iota(col_group[:].rearrange("p (g i) -> p g i", g=HALF_G), [[1, HALF_G], [0, SLICE]],
                           base=0, channel_multiplier=0).then_inc(s_const, 1)
            pool.wait_ge(s_const, 1)
            nc.gpsimd.affine_select(out=ident[:], in_=ident[:], compare_op=ALU.not_equal, fill=1.0, base=0,
                                    pattern=[[-1, P]], channel_multiplier=1).then_inc(s_ident, 1)

            def context_lo(b):
                pool.wait_ge(s_kc_hi, b + 1)
                nc.gpsimd.tensor_tensor(kt_lo[:, :, 0:S], ctxt_raw[:], f32(kt_hi[:, :, 0:S]),
                                        ALU.subtract).then_inc(s_kc_lo, 1)
                pool.wait_ge(s_vc_hi, b + 1)
                nc.gpsimd.tensor_tensor(v_lo[:, 0:ST, :], ctx_raw[:], f32(v_hi[:, 0:ST, :]),
                                        ALU.subtract).then_inc(s_vc_lo, 1)

            pool.wait_ge(s_gate_hi, 1)
            nc.gpsimd.tensor_tensor(gate_w[:, :, 1, :], gate_raw[:], f32(gate_w[:, :, 0, :]), ALU.subtract).then_inc(s_gate_lo, 1)
            context_lo(0)

            with pool.Fori(1, B) as b:
                context_lo(b)

            def wgu_low(p, j):
                pool.wait_ge(s_fw_hi[j], p + 1)
                nc.gpsimd.tensor_tensor(wgu_lo[:, j], wgu_raw[:], f32(wgu_hi[:, j]),
                                        ALU.subtract).then_inc(s_fw_lo[j], 1)

            def wd_low(p, j):
                pool.wait_ge(s_fd_hi[j], p + 1)
                nc.gpsimd.tensor_tensor(wd_lo[:, j], wd_raw[:], f32(wd_hi[:, j]),
                                        ALU.subtract).then_inc(s_fd_lo[j], 1)

            def act_low(p, j, c):
                n = p * 2 * CH + j * CH + c
                pool.wait_ge(s_at_hi, n + 1)
                nc.gpsimd.tensor_tensor(at_lo[:, j, c * BANK:(c + 1) * BANK], act[:, c % 2],
                                        f32(at_hi[:, j, c * BANK:(c + 1) * BANK]), ALU.subtract).then_inc(s_at_lo, 1)

            def turn(p, last):
                for j in range(2):
                    for c in range(CH):
                        act_low(p, j, c)
                        if c == 0:
                            wd_low(p, j)
                    if not last:
                        wgu_low(p + 1, j)

            def widen(b):
                pool.wait_ge(s_scal, b + 1)
                if b >= 4:
                    pool.wait_ge(s_bc, 2 * (b // 2 - 1))
                rows = wide[:, b // 2 % 2, b % 2 * ST:(b % 2 + 1) * ST].rearrange("p t j (g i) -> p (t j g) i", g=HALF_G)
                of_batch = scal_tok[:, b * ST:(b + 1) * ST].rearrange("p t j g -> p (t j g)")
                nc.gpsimd.tensor_copy(rows, of_batch.unsqueeze(2).broadcast_to([P, 2 * ST * HALF_G, SLICE])).then_inc(
                    s_wide, 1)

            wgu_low(0, 0)
            pool.wait_ge(s_y, NT)
            for b in range(4):
                widen(b)
            pool.wait_ge(s_mu_hi, 3)
            nc.gpsimd.tensor_tensor(mu[:, :, :, A_REST], mu_raw[:], f32(mu[:, :, :, A_HI]), ALU.subtract).then_inc(s_mu_lo, 1)
            wgu_low(0, 1)
            for b in range(4, B):
                widen(b)
            with pool.Fori(0, PAIRS - 1) as p:
                turn(p, False)
            turn(PAIRS - 1, True)

        @block.scalar
        def _(eng):
            nc.scalar.preload_act_table(ACT.Exp)
            eng.dma_start(gains_raw[:], gains).then_inc(s_gains, 16)
            eng.dma_start(inv_raw[:], inv_map).then_inc(s_small, 16)
            eng.dma_start(gate_raw[:], gate_t).then_inc(s_gate_in, 16)
            eng.wait_ge(s_gains, 16)
            nc.scalar.activation(gain[:], gains_raw[:], ACT.Tanh).then_inc(s_gain, 1)

            def weight_hi(m):
                eng.wait_ge(s_win[m], 16)
                nc.scalar.copy(w_hi(m), w_raw_of(m)).then_inc(s_w_hi, 1)

            def hi_of(ready, done, value, dst, src):
                eng.wait_ge(ready, value)
                nc.scalar.copy(dst, src).then_inc(done, 1)

            def norm_hi(b):
                for j in range(2):
                    hi_of(s_xnt, s_xnt_hi, 2 * b + j + 1, xnt_hi[:, 2 * j:2 * j + 2, :], bank[2 + j][:])

            def out_hi(b):
                for j in range(2):
                    hi_of(s_o, s_o_hi, 2 * b + j + 1, ot_hi[:, 2 * j:2 * j + 2, :], bank[4 + j][:])

            def logits_copy(r):
                eng.wait_ge(s_logit_t, r + 1)
                nc.scalar.copy(logit_t[:], bank[6][:, 0:S]).then_inc(s_logit_sb, 1)

            def token_exp(r):
                eng.wait_ge(s_centre, r + 1)
                nc.scalar.activation(prob[:], prob[:], ACT.Exp).then_inc(s_exp_tok, 1)

            def weights_copy(r):
                eng.wait_ge(s_wet, r + 1)
                nc.scalar.copy(we_t[:], bank[6][0:E, 0:S]).then_inc(s_wet_sb, 1)

            def soft_exp(r):
                eng.wait_ge(s_gcentre, r + 1)
                nc.scalar.activation(soft, soft, ACT.Exp).then_inc(s_exp_grp, 1)

            def soft_copies(r):
                soft_half = soft.rearrange("p t (h e) -> p (t h) e", h=2)
                eng.wait_ge(s_soft, r + 1)
                nc.scalar.copy(stack_tok[:].rearrange("p t h (k e) -> p (t h) k e", e=HALF_E)[:, :, 0:3, :],
                               soft_half.unsqueeze(2).broadcast_to([P, 2 * ST, 3, HALF_E])).then_inc(s_soft_hi, 1)

            def soft_t_copy(r):
                eng.wait_ge(s_st, r + 1)
                nc.scalar.copy(soft_t[:, :, bass.ds(r * S, S)],
                               bank[7][:].rearrange("p (h n) -> p h n", h=2)).then_inc(s_st_sb, 1)

            def iteration(b, part):
                r = b - 2
                if part.front:
                    for j in range(2):
                        hi_of(s_q, s_q_hi, 2 * b + j + 1, qt_hi[:, 2 * j:2 * j + 2, :], bank[j][:])
                def key_hi(j):
                    hi_of(s_k, s_k_hi, 2 * b + j + 1, kt_hi[:, 2 * j:2 * j + 2, S:KEYS], bank[2 + j][:])

                if part.front:
                    key_hi(0)
                if part.route:
                    for j in range(2):
                        hi_of(s_x2, s_x2_hi, 2 * r + j + 1, ot_hi[:, 2 * j:2 * j + 2, :], bank[4 + j][:])
                if part.front:
                    key_hi(1)
                    eng.wait_ge(s_ctxt_in, 16 * (b + 1))
                    nc.scalar.copy(kt_hi[:, :, 0:S], ctxt_raw[:]).then_inc(s_kc_hi, 1)
                if part.stack:
                    soft_exp(b - 3)
                    soft_copies(b - 3)
                if part.route:
                    logits_copy(r)
                if part.back:
                    out_hi(b - 1)
                if part.stack:
                    soft_t_copy(b - 3)
                if part.front:
                    eng.wait_ge(s_ctx_in, 16 * (b + 1))
                    nc.scalar.copy(v_hi[:, 0:ST, :], ctx_raw[:]).then_inc(s_vc_hi, 1)
                if part.route:
                    token_exp(r)
                if part.front:
                    for t in range(ST):
                        hi_of(s_v, s_v_hi, 2 * b + t + 1, v_hi[:, ST + t, :], bank[6 + t][:])
                    if part.first:
                        weight_hi(3)
                        eng.wait_ge(s_w_lo, 4)
                        eng.wait_ge(s_gate_lo, 1)
                    for t in range(ST):
                        eng.wait_ge(s_bias, 2 * b + t + 1)
                        nc.scalar.activation(probs[:, t, :], bank[t][:], ACT.Exp, bias=exp_bias[:, t:t + 1],
                                             scale=SCALE, accum_out=row_sum[:, t:t + 1]).then_inc(s_exp, 1)
                if part.route:
                    weights_copy(r)
                if part.next:
                    norm_hi(b + 1)
                if part.front:
                    for j in range(2):
                        hi_of(s_pt, s_pt_hi, 2 * b + j + 1, pt_hi[:, 2 * j:2 * j + 2, :], bank[6 + j][:])

            weight_hi(0)
            norm_hi(0)
            weight_hi(1)
            weight_hi(2)
            eng.wait_ge(s_gate_in, 16)
            nc.scalar.copy(gate_w[:, :, 0, :], gate_raw[:]).then_inc(s_gate_hi, 1)
            for b in range(LOOP[0]):
                iteration(b, Parts(b))
            with eng.Fori(*LOOP) as b:
                iteration(b, Parts())
            iteration(B - 1, Parts(B - 1))

            def wgu_high(p, j):
                eng.wait_ge(s_fw_in[j], 16 * (p + 1))
                nc.scalar.copy(wgu_hi[:, j], wgu_raw[:]).then_inc(s_fw_hi[j], 1)

            def second_hi(r):
                for j in range(2):
                    hi_of(s_x2, s_x2_hi, 2 * r + j + 1, x2t_hi[:, 2 * j:2 * j + 2, r * S:(r + 1) * S], bank[2 + j][:])

            def normed_again(c):
                eng.wait_ge(s_mv, 2 * c + 2)
                if c >= 2:
                    eng.wait_ge(s_x2t, DT * (c - 1))
                for t in range(4 * c, 4 * c + 4):
                    nc.scalar.activation(xn2[:, t % RING, :], xres[:, t, :], ACT.Identity, bias=mean_rstd[:, t:t + 1],
                                         scale=rstd[:, t:t + 1]).then_inc(s_xf, 1)

            def x2t_high(c, half):
                for h in (2 * half, 2 * half + 1):
                    hi_of(s_x2t, s_x2t_hi, DT * c + h + 1, x2t_hi[:, h, c * BANK:(c + 1) * BANK],
                          bank[X2T_BANK[c][h]][:])

            def scalars_copy(i):
                c, j = i // 2, i % 2
                eng.wait_ge(s_bc, i + 1)
                nc.scalar.copy(scalars[:, j, c * BANK:(c + 1) * BANK], bank[4 + j][:]).then_inc(s_bc_sb, 1)

            eng.wait_ge(s_exp, NT)
            normed_again(0)
            out_hi(B - 1)
            for half in range(2):
                x2t_high(0, half)
            second_hi(B - 2)
            wgu_high(0, 0)
            normed_again(1)
            logits_copy(B - 2)
            eng.wait_ge(s_mu, 16)
            eng.wait_ge(s_y, NT)
            for block in (A_HI, A_LO, A_HI_2):
                nc.scalar.copy(mu[:, :, :, block], mu_raw[:]).then_inc(s_mu_hi, 1)
            normed_again(2)
            token_exp(B - 2)
            second_hi(B - 1)
            x2t_high(1, 0)
            logits_copy(B - 1)
            x2t_high(1, 1)
            token_exp(B - 1)
            weights_copy(B - 2)
            soft_exp(B - 3)
            soft_copies(B - 3)
            wgu_high(0, 1)
            for half in range(2):
                x2t_high(2, half)
            soft_t_copy(B - 3)
            soft_exp(B - 2)
            soft_copies(B - 2)
            for i in range(2):
                scalars_copy(i)
            weights_copy(B - 1)
            soft_t_copy(B - 2)
            for i in range(2, 4):
                scalars_copy(i)
            soft_exp(B - 1)
            for i in range(4, 6):
                scalars_copy(i)
            soft_copies(B - 1)
            nc.scalar.preload_act_table(ACT.Silu)
            soft_t_copy(B - 1)

            def chunk(p, j, c):
                n = p * 2 * CH + j * CH + c
                eng.wait_ge(s_gate, n + 1)
                if j == 1 or c >= 2:
                    eng.wait_ge(s_at_lo, n - 1)
                nc.scalar.activation(act[:, c % 2], bank[2 * (c % 2)][:], ACT.Silu).then_inc(s_silu, 1)
                eng.wait_ge(s_act, n + 1)
                nc.scalar.copy(at_hi[:, j, c * BANK:(c + 1) * BANK], act[:, c % 2]).then_inc(s_at_hi, 1)

            def turn(p, last):
                for j in range(2):
                    for c in range(CH):
                        chunk(p, j, c)
                        if is_first(p) and j == 0 and c == 1:
                            for i in range(6, 8):
                                scalars_copy(i)
                        if c == 0:
                            eng.wait_ge(s_fd_in[j], 16 * (p + 1))
                            nc.scalar.copy(wd_hi[:, j], wd_raw[:]).then_inc(s_fd_hi[j], 1)
                    if not last:
                        wgu_high(p + 1, j)

            turn(0, False)
            with eng.Fori(1, PAIRS - 1) as p:
                turn(p, False)
            turn(PAIRS - 1, True)

        @block.vector
        def _(dve):
            norm_steps = [0]

            def apart():
                nc.vector.tensor_copy(scrap[:], ident[:, 0:1])

            def step(ins):
                norm_steps[0] += 1
                ins.then_inc(s_norm, 1)
                dve.wait_ge(s_norm, norm_steps[0])

            def rsqrt_of_variance(step, variance, y, width):
                v, z, bits = var_eps[:, 0:width], newton[:, 0:width], seed[:, 0:width]
                step(nc.vector.tensor_scalar(v, variance, EPS, None, ALU.add))
                step(nc.vector.tensor_scalar(bits, v.bitcast(I32), 1, None, ALU.logical_shift_right))
                step(nc.vector.tensor_scalar(bits, bits, -1.0, RSQRT_SEED, ALU.mult, ALU.add))
                step(nc.vector.tensor_copy(y, bits.bitcast(F32)))
                for _ in range(NEWTON):
                    step(nc.vector.tensor_tensor(z, y, y, ALU.mult))
                    step(nc.vector.scalar_tensor_tensor(out=z, in0=z, scalar=-0.5, in1=v, op0=ALU.mult, op1=ALU.mult))
                    step(nc.vector.scalar_tensor_tensor(out=y, in0=z, scalar=1.5, in1=y, op0=ALU.add, op1=ALU.mult))

            def norm_stats(t0, t1):
                for t in range(t0, t1):
                    last = nc.vector.bn_stats(stats_x[:, t, :], xres[:, t, :])
                step(last)
                for t in range(t0, t1):
                    last = nc.vector.bn_aggr(mv[:, t, :], stats_x[:, t, :])
                step(last)
                rsqrt_of_variance(step, mv[:, t0:t1, 1], rstd[:, t0:t1], t1 - t0)

            def norm_apply(b):
                for t in range(ST):
                    n = ST * b + t
                    nc.vector.tensor_scalar(xn[:, t, :], xres[:, bass.ds(n, 1), :], mv[:, bass.ds(n, 1), 0],
                                            rstd[:, bass.ds(n, 1)], ALU.subtract, ALU.mult).then_inc(s_xn, 1)

            def lo_of(hi_done, done, value, dst, src, hi):
                dve.wait_ge(hi_done, value)
                nc.vector.tensor_tensor(dst, src, f32(hi), ALU.subtract).then_inc(done, 1)

            def norm_lo(b):
                for j in range(2):
                    at = slice(2 * j, 2 * j + 2)
                    lo_of(s_xnt_hi, s_xnt_lo, 2 * b + j + 1, xnt_lo[:, at, :], bank[2 + j][:], xnt_hi[:, at, :])

            def out_lo(b):
                for j in range(2):
                    at = slice(2 * j, 2 * j + 2)
                    lo_of(s_o_hi, s_o_lo, 2 * b + j + 1, ot_lo[:, at, :], bank[4 + j][:], ot_hi[:, at, :])

            def weight_lo(m):
                lo_of(s_w_hi, s_w_lo, m + 1, w_lo(m), w_raw_of(m), w_hi(m))

            def residual(b, t):
                n = ST * b + t
                row = xres[:, bass.ds(n, 1), :]
                dve.wait_ge(s_y, n + 1)
                nc.vector.scalar_tensor_tensor(out=row, in0=bank[4 + t][:], scalar=out_coef[:, t:t + 1], in1=row,
                                               op0=ALU.mult, op1=ALU.add).then_inc(s_x1, 1)
                dve.wait_ge(s_x1, n + 1)
                apart()
                nc.vector.bn_stats(stats_2[:, t, :], row).then_inc(s_stat, 1)

            norm2_step = Steps(dve, s_norm2, NORM_STEPS)
            route_step = [Steps(dve, s_route[i], ROUTE_STEPS[i]) for i in range(3)]

            def norm2(r):
                dve.wait_ge(s_stat, ST * (r + 1))
                norm2_step.begin(r)
                apart()
                for t in range(ST):
                    last = nc.vector.bn_aggr(mv_2[:, t, :], stats_2[:, t, :])
                norm2_step(last)
                rsqrt_of_variance(norm2_step, mv_2[:, :, 1], rstd_2[:], ST)
                norm2_step.end()
                for t in range(ST):
                    n = ST * r + t
                    nc.vector.tensor_scalar(xn[:, t, :], xres[:, bass.ds(n, 1), :], mv_2[:, t, 0:1], rstd_2[:, t:t + 1],
                                            ALU.subtract, ALU.mult).then_inc(s_xn2, 1)
                nc.vector.scalar_tensor_tensor(out=mean_rstd[:, bass.ds(ST * r, ST)], in0=mv_2[:, :, 0], scalar=-1.0,
                                               in1=rstd_2[:], op0=ALU.mult, op1=ALU.mult)
                nc.vector.tensor_copy(rstd[:, bass.ds(ST * r, ST)], rstd_2[:]).then_inc(s_mv, 1)

            def per_row(v, n):
                return v.unsqueeze(2).broadcast_to([P, v.shape[1], n])

            def route_centre(r, logits_bank):
                route = route_step[0]
                route.begin(r)
                logits = bank[logits_bank][:, 0:ST * E].rearrange("p (t e) -> p t e", e=E)
                dve.wait_ge(s_logit, r + 1)
                route(nc.vector.tensor_reduce(tok_max[:], logits, AX.X, ALU.max))
                route.end()
                nc.vector.tensor_tensor(prob[:], logits, per_row(tok_max[:], E), ALU.subtract).then_inc(s_centre, 1)

            def route_top(r):
                route = route_step[1]
                route.begin(r)
                dve.wait_ge(s_exp_tok, r + 1)
                route(nc.vector.tensor_reduce(tok_sum[:], prob[:], AX.X, ALU.add))
                route(nc.vector.reciprocal(tok_inv[:], tok_sum[:]))
                route(nc.vector.tensor_tensor(prob[:], prob[:], per_row(tok_inv[:], E), ALU.mult))
                apart()
                for t in range(ST):
                    last = nc.vector.max(top8[:, t, :], prob[:, t, :])
                route(last)
                apart()
                for t in range(ST):
                    last = nc.vector.match_replace(rest[:, t, :], top8[:, t, :], prob[:, t, :], 0.0)
                route(last)
                route.end()
                nc.vector.tensor_tensor(rest[:], prob[:], rest[:], ALU.subtract).then_inc(s_we, 1)

            def route_flat(r):
                dve.wait_ge(s_flat, r + 1)
                nc.vector.tensor_copy(flat, bank[7][:, 0:ST * E].rearrange("p (t e) -> p t e", e=E)).then_inc(s_flat_sb, 1)

            def route_soft(r):
                by_group = flat.rearrange("p t (g s) -> p (t g) s", s=GS)
                soft_group = soft.rearrange("p t (g s) -> p (t g) s", s=GS)
                scal_flat = scal[:].rearrange("p t h g -> p (t h g)")
                dve.wait_ge(s_flat_sb, r + 1)
                route = route_step[2]
                route.begin(r)
                route(nc.vector.tensor_scalar(soft, flat, 0.0, NEG_INF, ALU.is_equal, ALU.mult))
                route(nc.vector.tensor_tensor(soft, soft, flat, ALU.add))
                route(nc.vector.tensor_reduce(grp_max[:], soft_group, AX.X, ALU.max))
                nc.vector.tensor_tensor(soft_group, soft_group, per_row(grp_max[:], GS),
                                        ALU.subtract).then_inc(s_gcentre, 1)
                route(nc.vector.tensor_reduce(scal_flat, by_group, AX.X, ALU.add))
                nc.vector.tensor_scalar(scal_tok[:, bass.ds(r * ST, ST)].rearrange("p t h g -> p (t h g)"), scal_flat,
                                        gain[:, 1:2], None, ALU.mult).then_inc(s_scal, 1)
                dve.wait_ge(s_exp_grp, r + 1)
                route(nc.vector.tensor_reduce(grp_sum[:], soft_group, AX.X, ALU.add))
                route(nc.vector.reciprocal(grp_inv[:], grp_sum[:]))
                route.end()
                nc.vector.tensor_tensor(soft_group, soft_group, per_row(grp_inv[:], GS),
                                        ALU.mult).then_inc(s_soft, 1)
                dve.wait_ge(s_soft_hi, r + 1)
                nc.vector.tensor_tensor(stack_tok[:, :, :, A_HI_2],
                                        soft.rearrange("p t (h e) -> p t h e", h=2),
                                        f32(stack_tok[:, :, :, A_HI]), ALU.subtract).then_inc(s_stack, 1)

            def coefficient(b):
                dve.wait_ge(s_exp, 2 * b + 2)
                nc.vector.reciprocal(row_inv[:], row_sum[:]).then_inc(s_rinv, 1)
                dve.wait_ge(s_rinv, b + 1)
                nc.vector.tensor_scalar(out_coef[:], row_inv[:], gain[:, 0:1], None, ALU.mult).then_inc(s_coef, 1)

            def iteration(b, part):
                r = b - 2
                if part.front:
                    for j in range(2):
                        at = slice(2 * j, 2 * j + 2)
                        lo_of(s_q_hi, s_q_lo, 2 * b + j + 1, qt_lo[:, at, :], bank[j][:], qt_hi[:, at, :])
                def key_lo(j):
                    at = slice(2 * j, 2 * j + 2)
                    lo_of(s_k_hi, s_k_lo, 2 * b + j + 1, kt_lo[:, at, S:KEYS], bank[2 + j][:], kt_hi[:, at, S:KEYS])

                if part.front:
                    key_lo(0)
                if part.route:
                    for j in range(2):
                        at = slice(2 * j, 2 * j + 2)
                        lo_of(s_x2_hi, s_x2_lo, 2 * r + j + 1, ot_lo[:, at, :], bank[4 + j][:], ot_hi[:, at, :])
                if part.front:
                    key_lo(1)
                if part.first:
                    dve.wait_ge(s_xr, 16)
                    norm_stats(ST, 2 * ST)
                if part.stack:
                    route_soft(b - 3)
                if part.next:
                    norm_apply(b + 1)
                if part.back:
                    out_lo(b - 1)
                if part.route:
                    route_centre(r, 0)
                if part.front:
                    for t in range(ST):
                        lo_of(s_v_hi, s_v_lo, 2 * b + t + 1, v_lo[:, ST + t, :], bank[6 + t][:], v_hi[:, ST + t, :])
                if part.first:
                    weight_lo(3)
                if part.route:
                    route_top(r)
                if part.front:
                    for t in range(ST):
                        dve.wait_ge(s_scores, 2 * b + t + 1)
                        nc.vector.tensor_reduce(neg_max[:, t:t + 1], bank[t][:], AX.X, ALU.max,
                                                negate=True).then_inc(s_max, 1)
                        dve.wait_ge(s_max, 2 * b + t + 1)
                        nc.vector.tensor_scalar(exp_bias[:, t:t + 1], neg_max[:, t:t + 1], SCALE, None,
                                                ALU.mult).then_inc(s_bias, 1)
                if part.next:
                    norm_lo(b + 1)
                if part.back:
                    dve.wait_ge(s_coef, b)
                    residual(b - 1, 0)
                if part.route:
                    route_flat(r)
                if part.back and part.next:
                    residual(b - 1, 1)
                    norm2(b - 1)
                if part.next:
                    coefficient(b)
                for j in range(2):
                    at = slice(2 * j, 2 * j + 2)
                    lo_of(s_pt_hi, s_pt_lo, 2 * b + j + 1, pt_lo[:, at, :], bank[6 + j][:], pt_hi[:, at, :])
                if not part.next:
                    residual(b - 1, 1)
                    coefficient(b)
                    norm2(b - 1)
                if part.first:
                    norm_stats(2 * ST, NT)

            dve.wait_ge(s_x0, 16)
            dve.wait_ge(s_ident, 1)
            norm_stats(0, ST)
            norm_apply(0)
            weight_lo(0)
            norm_lo(0)
            weight_lo(1)
            weight_lo(2)
            dve.wait_ge(s_const, 4)
            step(nc.vector.tensor_scalar(row_group_i[:], row_i[:], HALF_E - 1, 3, ALU.bitwise_and,
                                         ALU.logical_shift_right))
            step(nc.vector.tensor_copy(row_group[:], row_group_i[:]))
            step(nc.vector.tensor_scalar(group_mask[:], col_group[:], row_group[:, 0:1], None, ALU.is_equal))
            dve.wait_ge(s_small, 16)
            step(nc.vector.tensor_copy(inv_f[:], inv_raw[:]))
            step(nc.vector.tensor_scalar(inv_neg[:], inv_f[:], 0.0, float(E), ALU.is_lt, ALU.mult))
            step(nc.vector.tensor_tensor(inv_f[:], inv_f[:], inv_neg[:], ALU.add))
            step(nc.vector.tensor_copy(expert_f[:], expert_i[:]))
            step(nc.vector.tensor_scalar(pick[:], inv_f[:], expert_f[:, 0:1], None, ALU.is_equal))
            step(nc.vector.tensor_tensor(fold[:], ident[:, 0:E], ident[:, E:2 * E], ALU.add))
            dve.wait_ge(s_gain, 1)
            for b in range(LOOP[0]):
                iteration(b, Parts(b))
            with dve.Fori(*LOOP) as b:
                iteration(b, Parts())
            iteration(B - 1, Parts(B - 1))

            def second_lo(r):
                for j in range(2):
                    at, tokens = slice(2 * j, 2 * j + 2), slice(r * S, (r + 1) * S)
                    lo_of(s_x2_hi, s_x2_lo, 2 * r + j + 1, x2t_lo[:, at, tokens], bank[2 + j][:], x2t_hi[:, at, tokens])

            def x2t_low(c, half):
                at = slice(c * BANK, (c + 1) * BANK)
                for h in (2 * half, 2 * half + 1):
                    lo_of(s_x2t_hi, s_x2t_lo, DT * c + h + 1, x2t_lo[:, h, at], bank[X2T_BANK[c][h]][:],
                          x2t_hi[:, h, at])

            out_lo(B - 1)
            for half in range(2):
                x2t_low(0, half)
            second_lo(B - 2)
            dve.wait_ge(s_coef, B)
            for t in range(ST):
                residual(B - 1, t)
            norm2(B - 1)
            route_centre(B - 2, 7)
            second_lo(B - 1)
            route_top(B - 2)
            for half in range(2):
                x2t_low(1, half)
            dve.wait_ge(s_we, B - 1)
            route_centre(B - 1, 7)
            route_soft(B - 3)
            dve.wait_ge(s_wet, B - 1)
            route_top(B - 1)
            route_flat(B - 2)
            for half in range(2):
                x2t_low(2, half)
            dve.wait_ge(s_st, B - 2)
            route_soft(B - 2)
            route_flat(B - 1)
            dve.wait_ge(s_st, B - 1)
            route_soft(B - 1)

            def a_tile(p, j):
                k = 2 * p + j + 1
                columns = group_mask[:].unsqueeze(1).broadcast_to([STACK, 2, P])
                dve.wait_ge(s_a, k)
                nc.vector.tensor_tensor(a_tmp[:], bank[4 + j][:, 0:2 * P].rearrange("p (m r) -> p m r", m=2),
                                        columns, ALU.mult).then_inc(s_a_masked, 1)
                dve.wait_ge(s_a_masked, k)
                nc.vector.tensor_copy(a_stack[:, j], a_tmp[:]).then_inc(s_a_hi, 1)
                dve.wait_ge(s_a_hi, k)
                nc.vector.tensor_tensor(a_stack[A_LO, j], a_tmp[A_LO], f32(a_stack[A_LO, j]),
                                        ALU.subtract).then_inc(s_a_st, 1)

            def chunk(p, j, c):
                n = p * 2 * CH + j * CH + c
                s = c % 2
                dve.wait_ge(s_silu, n + 1)
                dve.wait_ge(s_up, n + 1)
                nc.vector.tensor_tensor(act[:, s], act[:, s], bank[2 * s + 1][:], ALU.mult).then_inc(s_prod, 1)
                dve.wait_ge(s_prod, n + 1)
                if is_first(p) and j == 0:
                    dve.wait_ge(s_bc_sb, 6 if c < 3 else 8)
                nc.vector.tensor_tensor(act[:, s], act[:, s], scalars[:, j, c * BANK:(c + 1) * BANK],
                                        ALU.mult).then_inc(s_act, 1)

            def turn(p):
                for j in range(2):
                    if not is_first(p):
                        a_tile(p, j)
                    for c in range(CH):
                        chunk(p, j, c)
                for t in range(NT):
                    dve.wait_ge(s_down, NT * p + t + 1)
                    nc.vector.tensor_tensor(xres[:, t, :], xres[:, t, :], bank[6 + t % 2][:], ALU.add).then_inc(s_res, 1)

            for j in range(2):
                a_tile(0, j)
                dve.wait_ge(s_a_st, j + 1)
            turn(0)
            with dve.Fori(1, PAIRS) as p:
                turn(p)

        @block.tensor
        def _(pe):
            def mm(out_ap, pairs):
                return accumulate(nc, out_ap, pairs)

            def project_t(m, b0, ready, j):
                for e in (2 * j, 2 * j + 1):
                    last = mm(bank[b0 + e // 2][:, (e % 2) * S:(e % 2 + 1) * S],
                              split_products(lambda k: w_hi(m)[:, k, e * P:(e + 1) * P], lambda k: w_lo(m)[:, k, e * P:(e + 1) * P],
                                             lambda k: xnt_hi[:, k, :], lambda k: xnt_lo[:, k, :], range(DT)))
                    if e % 2:
                        last.then_inc(ready, 1)

            def transposes(src, b0, ready):
                for h in range(DT):
                    for t in range(ST):
                        last = nc.tensor.transpose(bank[b0 + h // 2][:, (h % 2) * S + t * P:(h % 2) * S + (t + 1) * P],
                                                   src[:, t, h * P:(h + 1) * P], ident[:])
                    if h % 2:
                        last.then_inc(ready, 1)

            def norm_transposes(b):
                pe.wait_ge(s_xn, 2 * b + 2)
                transposes(xn, 2, s_xnt)

            def attend(b, follows_output=False):
                pe.wait_ge(s_pt_lo, 2 * b + 2)
                pe.wait_ge(s_v_lo, 2 * b + 2)
                pe.wait_ge(s_vc_lo, b + 1)
                for d in range(DT):
                    if d == 2 and follows_output:
                        pe.wait_ge(s_x1, ST * b)
                    at = slice(d * P, (d + 1) * P)
                    last = mm(bank[4 + d // 2][:, (d % 2) * S:(d % 2 + 1) * S],
                              split_products(lambda k: v_hi[:, k, at], lambda k: v_lo[:, k, at],
                                             lambda k: pt_hi[:, k, :], lambda k: pt_lo[:, k, :], range(KT)))
                    if d % 2:
                        last.then_inc(s_o, 1)

            def output(b, t):
                at = slice(t * P, (t + 1) * P)
                mm(bank[4 + t][:], split_products(lambda k: ot_hi[:, k, at], lambda k: ot_lo[:, k, at],
                                                  lambda k: w_hi(3)[:, k, :], lambda k: w_lo(3)[:, k, :],
                                                  range(DT))).then_inc(s_y, 1)

            def values(t):
                at = slice(t * P, (t + 1) * P)
                mm(bank[6 + t][:], split_products(lambda k: xnt_hi[:, k, at], lambda k: xnt_lo[:, k, at],
                                                  lambda k: w_hi(2)[:, k, :], lambda k: w_lo(2)[:, k, :],
                                                  range(DT))).then_inc(s_v, 1)

            def stack_transposes(r):
                pe.wait_ge(s_stack, r + 1)
                for h in range(2):
                    for t in range(ST):
                        last = nc.tensor.transpose(bank[7][:, h * S + t * P:h * S + (t + 1) * P],
                                                   f32(stack_tok[:, t, h, :]), ident[:])
                last.then_inc(s_st, 1)

            def logits(r, hi, lo):
                pe.wait_ge(s_x2_lo, 2 * r + 2)
                pe.wait_ge(s_gate_lo, 1)
                for k in range(DT):
                    for n, part in enumerate((hi, lo)):
                        last = nc.tensor.matmul(bank[6][:, 0:S], gate_w[:, k], part(k), start=k + n == 0,
                                                stop=k == DT - 1 and n == 1)
                last.then_inc(s_logit_t, 1)

            def logit_folds(logits_bank):
                for t in range(ST):
                    last = nc.tensor.matmul(bank[logits_bank][:, t * E:(t + 1) * E], logit_t[:, t * P:(t + 1) * P], fold[:],
                                            start=True, stop=True)
                last.then_inc(s_logit, 1)

            def weight_transposes():
                for t in range(ST):
                    last = nc.tensor.transpose(bank[6][0:E, t * P:(t + 1) * P], rest[:, t, :], ident[:])
                last.then_inc(s_wet, 1)

            def flat_products():
                for t in range(ST):
                    last = nc.tensor.matmul(bank[7][:, t * E:(t + 1) * E], we_t[:, t * P:(t + 1) * P], pick[:],
                                            start=True, stop=True)
                last.then_inc(s_flat, 1)

            def iteration(b, part):
                r = b - 2
                pe.wait_ge(s_xnt_lo, 2 * b + 2)
                if part.first:
                    pe.wait_ge(s_w_lo, 1)
                else:
                    pe.wait_ge(s_exp, 2 * b)
                for j in range(2):
                    project_t(0, 0, s_q, j)
                if part.first:
                    pe.wait_ge(s_w_lo, 2)
                project_t(1, 2, s_k, 0)
                if part.route:
                    pe.wait_ge(s_xn2, 2 * r + 2)
                    transposes(xn, 4, s_x2)
                project_t(1, 2, s_k, 1)
                if part.route:
                    pe.wait_ge(s_pt_lo, 2 * b)
                    logits(r, lambda k: ot_hi[:, k, :], lambda k: ot_lo[:, k, :])
                if part.back:
                    attend(b - 1)
                if part.stack:
                    stack_transposes(b - 3)
                if part.route:
                    pe.wait_ge(s_logit_sb, r + 1)
                    pe.wait_ge(s_q_lo, 2 * b + 2)
                if part.first:
                    pe.wait_ge(s_w_lo, 3)
                else:
                    pe.wait_ge(s_pt_lo, 2 * b)
                values(0)
                if part.route:
                    logit_folds(0)
                if part.stack:
                    pe.wait_ge(s_st_sb, b - 2)
                values(1)
                pe.wait_ge(s_q_lo, 2 * b + 2)
                pe.wait_ge(s_k_lo, 2 * b + 2)
                pe.wait_ge(s_kc_lo, b + 1)
                if part.route:
                    pe.wait_ge(s_centre, r + 1)
                for t in range(ST):
                    at = slice(t * P, (t + 1) * P)
                    mm(bank[t][:], split_products(lambda k: qt_hi[:, k, at], lambda k: qt_lo[:, k, at],
                                                  lambda k: kt_hi[:, k, :], lambda k: kt_lo[:, k, :],
                                                  range(DT))).then_inc(s_scores, 1)
                if part.route:
                    pe.wait_ge(s_v_lo, 2 * b + 1)
                    pe.wait_ge(s_we, r + 1)
                    if part.next:
                        norm_transposes(b + 1)
                    weight_transposes()
                elif part.next:
                    norm_transposes(b + 1)
                if part.back:
                    pe.wait_ge(s_o_lo, 2 * b)
                    pe.wait_ge(s_w_lo, 4)
                    output(b - 1, 0)
                if part.route:
                    pe.wait_ge(s_wet_sb, r + 1)
                    pe.wait_ge(s_v_lo, 2 * b + 2)
                    flat_products()
                if part.back and part.next:
                    output(b - 1, 1)
                pe.wait_ge(s_exp, 2 * b + 2)
                pe.wait_ge(s_v_lo, 2 * b + 2)
                if part.route:
                    pe.wait_ge(s_flat_sb, r + 1)
                transposes(probs, 6, s_pt)
                if not part.next:
                    output(b - 1, 1)

            pe.wait_ge(s_ident, 1)
            norm_transposes(0)
            for b in range(LOOP[0]):
                iteration(b, Parts(b))
            with pe.Fori(*LOOP) as b:
                iteration(b, Parts())
            iteration(B - 1, Parts(B - 1))

            def second_transposes(r):
                pe.wait_ge(s_xn2, 2 * r + 2)
                transposes(xn, 2, s_x2)

            def second_tokens(r):
                tokens = slice(r * S, (r + 1) * S)
                return lambda k: x2t_hi[:, k, tokens], lambda k: x2t_lo[:, k, tokens]

            def x2t_transposes(c, half):
                pe.wait_ge(s_xf, 4 * c + 4)
                for h in (2 * half, 2 * half + 1):
                    m = DT * c + h
                    if m >= DT + 2 and h >= 2:
                        pe.wait_ge(s_x2t_lo, m - 1)
                    for t in range(4):
                        last = nc.tensor.transpose(bank[X2T_BANK[c][h]][:, t * P:(t + 1) * P],
                                                   xn2[:, (4 * c + t) % RING, h * P:(h + 1) * P], ident[:])
                    last.then_inc(s_x2t, 1)

            def spread(i):
                c, j = i // 2, i % 2
                pe.wait_ge(s_wide, 2 * c + 2)
                for t in range(4):
                    last = nc.tensor.transpose(bank[4 + j][:, t * P:(t + 1) * P], wide[:, c % 2, t, j, :], ident[:])
                last.then_inc(s_bc, 1)

            def a_products(j):
                for k in range(DT):
                    for n, w in enumerate((wgu_hi, wgu_lo)):
                        last = nc.tensor.matmul(bank[4 + j][:, 0:2 * P], mu[:, k, j, :], w[:, j, k, :], start=k + n == 0,
                                                stop=k == DT - 1 and n == 1)
                last.then_inc(s_a, 1)

            def token_products(j, c, m):
                at, rows = slice(c * BANK, (c + 1) * BANK), slice(m * P, (m + 1) * P)
                pairs = split_products(lambda k: wgu_hi[:, j, k, rows], lambda k: wgu_lo[:, j, k, rows],
                                       lambda k: x2t_hi[:, k, at], lambda k: x2t_lo[:, k, at], range(DT))
                for q, (stationary, moving) in enumerate(pairs):
                    nc.tensor.matmul(bank[2 * (c % 2) + m][:], stationary, moving, start=q == 0, stop=False)

            def soft_product(j, c, m):
                nc.tensor.matmul(bank[2 * (c % 2) + m][:], a_stack[:, j, m, :],
                                 soft_t[:, j, c * BANK:(c + 1) * BANK], start=False,
                                 stop=True).then_inc((s_gate, s_up)[m], 1)

            def chunk(p, j, c):
                n = p * 2 * CH + j * CH + c
                if j == 1 or c >= 2:
                    pe.wait_ge(s_prod, n - 1)
                if c == 0:
                    pe.wait_ge(s_fw_lo[j], p + 1)
                for m in range(2):
                    token_products(j, c, m)
                    if c == 0 and m == 0 and not is_first(p):
                        a_products(j)
                    if c > 0:
                        soft_product(j, c, m)
                if c == 0:
                    pe.wait_ge(s_a_st, 2 * p + j + 1)
                    for m in range(2):
                        soft_product(j, c, m)

            def turn(p):
                for j in range(2):
                    for c in range(CH):
                        if not (is_first(p) and j == 0 and c < 2):
                            chunk(p, j, c)
                for j in range(2):
                    pe.wait_ge(s_fd_lo[j], p + 1)
                for t in range(NT):
                    pe.wait_ge(s_at_lo, 2 * CH * p + CH + t // 4 + 1)
                    if t >= 2:
                        pe.wait_ge(s_res, NT * p + t - 1)
                    at = slice(t * P, (t + 1) * P)
                    mm(bank[6 + t % 2][:], split_products(lambda k: at_hi[:, k, at], lambda k: at_lo[:, k, at],
                                                          lambda k: wd_hi[:, k, :], lambda k: wd_lo[:, k, :],
                                                          range(2))).then_inc(s_down, 1)

            attend(B - 1, follows_output=True)
            for half in range(2):
                x2t_transposes(0, half)
            second_transposes(B - 2)
            pe.wait_ge(s_o_lo, NT)
            for t in range(ST):
                output(B - 1, t)
            pe.wait_ge(s_x2t_lo, DT)
            logits(B - 2, *second_tokens(B - 2))
            pe.wait_ge(s_fw_lo[0], 1)
            token_products(0, 0, 0)
            pe.wait_ge(s_logit_sb, B - 1)
            logit_folds(7)
            pe.wait_ge(s_x2_lo, NT - 2)
            second_transposes(B - 1)
            x2t_transposes(1, 0)
            token_products(0, 0, 1)
            logits(B - 1, *second_tokens(B - 1))
            x2t_transposes(1, 1)
            pe.wait_ge(s_logit_sb, B)
            pe.wait_ge(s_centre, B - 1)
            logit_folds(7)
            pe.wait_ge(s_we, B - 1)
            weight_transposes()
            pe.wait_ge(s_x2t_lo, 2 * DT)
            token_products(0, 1, 0)
            pe.wait_ge(s_wet_sb, B - 1)
            pe.wait_ge(s_centre, B)
            flat_products()
            for half in range(2):
                x2t_transposes(2, half)
            pe.wait_ge(s_flat_sb, B - 1)
            stack_transposes(B - 3)
            pe.wait_ge(s_we, B)
            weight_transposes()
            token_products(0, 1, 1)
            pe.wait_ge(s_x2t_lo, 3 * DT)
            for i in range(2):
                spread(i)
            pe.wait_ge(s_wet_sb, B)
            pe.wait_ge(s_st_sb, B - 2)
            flat_products()
            pe.wait_ge(s_flat_sb, B)
            stack_transposes(B - 2)
            for i in range(2, 6):
                pe.wait_ge(s_bc_sb, i - 1)
                spread(i)
            pe.wait_ge(s_mu_lo, 1)
            for j in range(2):
                pe.wait_ge(s_fw_lo[j], 1)
                pe.wait_ge(s_bc_sb, 5 + j)
                a_products(j)
            pe.wait_ge(s_st_sb, B - 1)
            stack_transposes(B - 1)
            pe.wait_ge(s_a_st, 1)
            for c in range(2):
                for m in range(2):
                    soft_product(0, c, m)
            pe.wait_ge(s_st_sb, B)
            for i in range(6, 8):
                pe.wait_ge(s_a_st, i - 5)
                spread(i)

            turn(0)
            with pe.Fori(1, PAIRS) as p:
                turn(p)


def kernel(**inputs):
    import numpy as np
    import concourse.bacc as bacc
    from concourse.bass_utils import run_bass_kernel_spmd

    given = {name: np.asarray(value) for name, value in inputs.items()}

    def by_k_tile(w):
        return w.T.reshape(DT, P, w.shape[0]).transpose(1, 0, 2)

    w_qkvo = np.stack([by_k_tile(given[f"L0_xattn_w{n}"]) for n in "qkvo"])
    ctx = given["ctx_2048"]
    ctx_t = ctx.transpose(0, 2, 1).reshape(B, DT, P, S).transpose(0, 2, 1, 3)

    def inner_rows(w):
        return w.reshape(2, HALF_G, PAIRS, SLICE, D).transpose(2, 0, 1, 3, 4).reshape(PAIRS, 2, P, D)

    gate_up = np.stack([inner_rows(given[f"L0_ffn_{n}_proj_w"]) for n in ("gate", "up")], axis=2)
    gate_up = gate_up.reshape(PAIRS, 2, 2, P, DT, P).transpose(0, 1, 5, 4, 2, 3).reshape(PAIRS, 2, P, DT, 2 * P)
    down = inner_rows(given["L0_ffn_down_proj_w"].transpose(0, 2, 1))
    mask_up = given["L0_ffn_mask_up_w"].transpose(1, 0, 2).reshape(DT, P, 2, HALF_E).transpose(1, 0, 2, 3)
    arrays = {
        "x": given["x"],
        "ctx": ctx,
        "ctx_t": ctx_t,
        "w_qkvo": w_qkvo,
        "w_gate_up": gate_up,
        "w_down": down,
        "mask_up": mask_up,
        "gate_t": by_k_tile(given["L0_ffn_gate_w"]),
        "inv_map": np.broadcast_to(given["L0_ffn_inv_map"].reshape(1, E), (E, E)),
        "gains": np.broadcast_to(np.concatenate([given["g_xattn"], given["g_ffn"]]), (P, 2)),
    }
    arrays = {f"in_{name}": np.ascontiguousarray(value) for name, value in arrays.items()}
    nc = bacc.Bacc("TRN2", target_bir_lowering=False, num_devices=1)
    args = [nc.dram_tensor(name, value.shape, mybir.dt.from_np(value.dtype), kind="ExternalInput").ap()
            for name, value in arrays.items()]
    out = nc.dram_tensor("out", (B, S, D), F32, kind="ExternalOutput").ap()
    layer_program(nc, *args, out)
    result = run_bass_kernel_spmd(nc, [arrays], core_ids=[0])
    return result.results[0]["out"]
```
